# Optimizing a Trainium2 kernel written in Bass

```python
import numpy as np
import jax
import jax.numpy as jnp

def _softmax(x, axis=-1):
    return jax.nn.softmax(x, axis=axis)

def _gelu(x):
    return jax.nn.gelu(x, approximate=True)

def _silu(x):
    return jax.nn.silu(x)

def _sigmoid(x):
    return jax.nn.sigmoid(x)

def _layernorm(x, axis=-1, eps=1e-05):
    m = jnp.mean(x, axis=axis, keepdims=True)
    v = jnp.var(x, axis=axis, keepdims=True)
    return (x - m) / jnp.sqrt(v + eps)

def _scatter_add(tgt, idx, src, axis=0):
    return tgt.at[idx].add(src)

def _segment_sum(src, seg, n):
    return jax.ops.segment_sum(src, seg, n)
kernel_name = 'mk_prb_d1_jaxref_r8_0e0523'

def setup_inputs(seed: int=0):
    np.random.seed(seed)
    _w = jnp.asarray

    def _L0_attn_setup():
        import math
        import jax, jax.numpy as jnp
        import numpy as np
        B, T, E, H, L = (2, 256, 128, 16, 128)
        key = jax.random.key(seed)
        ks = jax.random.split(key, 11)
        w = lambda k, shape: jax.random.normal(k, shape, jnp.float32) * 0.02
        return {'x': jax.random.normal(ks[0], (B, T, E), jnp.float32), 'Wq': w(ks[1], (E, E)), 'bq': jnp.zeros((E,), jnp.float32), 'Wk': w(ks[2], (E, E)), 'bk': jnp.zeros((E,), jnp.float32), 'Wv': w(ks[3], (E, E)), 'bv': jnp.zeros((E,), jnp.float32), 'Wl': w(ks[4], (E, L)), 'bl': jnp.zeros((L,), jnp.float32), 'Wo': w(ks[5], (L, E)), 'bo': jnp.zeros((E,), jnp.float32)}
    _L0_attn_in = _L0_attn_setup()

    def _L0_ffn_setup():
        import jax, jax.numpy as jnp
        import numpy as np
        TOP_K = 2
        TEMP = 0.9
        EPS = 1e-05
        B, S, D, F, E = (2, 256, 128, 512, 8)

        def _moe_forward(x, gate_w, gate_b, w1, b1, w2, b2, ln_g, ln_b):
            logits = (x @ gate_w + gate_b) / TEMP
            topk_vals, topk_idx = jax.lax.top_k(logits, TOP_K)
            keep = jax.nn.one_hot(topk_idx, E, dtype=jnp.bool_).any(-2)
            masked = jnp.where(keep, logits, -jnp.inf)
            gate_probs = jax.nn.softmax(masked, axis=-1)
            h = jnp.einsum('bsd,edf->bsef', x, w1) + b1
            h = jax.nn.gelu(h, approximate=False)
            expert_out = jnp.einsum('bsef,efd->bsed', h, w2) + b2
            out = jnp.einsum('bse,bsed->bsd', gate_probs, expert_out)
            mu = out.mean(-1, keepdims=True)
            var = out.var(-1, keepdims=True)
            out = (out - mu) / jnp.sqrt(var + EPS) * ln_g + ln_b
            return out
        key = jax.random.key(seed)
        ks = jax.random.split(key, 4)
        scale_in = 1.0 / np.sqrt(D)
        scale_ff = 1.0 / np.sqrt(F)
        return {'x': jax.random.normal(ks[0], (B, S, D), jnp.float32), 'gate_w': jax.random.normal(ks[1], (D, E), jnp.float32) * scale_in, 'gate_b': jnp.zeros((E,), jnp.float32), 'w1': jax.random.normal(ks[2], (E, D, F), jnp.float32) * scale_in, 'b1': jnp.zeros((E, F), jnp.float32), 'w2': jax.random.normal(ks[3], (E, F, D), jnp.float32) * scale_ff, 'b2': jnp.zeros((E, D), jnp.float32), 'ln_g': jnp.ones((D,), jnp.float32), 'ln_b': jnp.zeros((D,), jnp.float32)}
    _L0_ffn_in = _L0_ffn_setup()
    _d = {'L0_attn_x': _L0_attn_in['x'], 'L0_attn_Wq': _L0_attn_in['Wq'], 'L0_attn_bq': _L0_attn_in['bq'], 'L0_attn_Wk': _L0_attn_in['Wk'], 'L0_attn_bk': _L0_attn_in['bk'], 'L0_attn_Wv': _L0_attn_in['Wv'], 'L0_attn_bv': _L0_attn_in['bv'], 'L0_attn_Wl': _L0_attn_in['Wl'], 'L0_attn_bl': _L0_attn_in['bl'], 'L0_attn_Wo': _L0_attn_in['Wo'], 'L0_attn_bo': _L0_attn_in['bo'], 'L0_ffn_gate_w': _L0_ffn_in['gate_w'], 'L0_ffn_gate_b': _L0_ffn_in['gate_b'], 'L0_ffn_w1': _L0_ffn_in['w1'], 'L0_ffn_b1': _L0_ffn_in['b1'], 'L0_ffn_w2': _L0_ffn_in['w2'], 'L0_ffn_b2': _L0_ffn_in['b2'], 'L0_ffn_ln_g': _L0_ffn_in['ln_g'], 'L0_ffn_ln_b': _L0_ffn_in['ln_b']}
    _x0 = _d['L0_attn_x']
    _d['L0_attn_x'] = jax.random.normal(jax.random.fold_in(jax.random.key(seed), 1), (32, 256, 128), dtype=_x0.dtype)
    del _x0
    return _d

def reference(L0_attn_x, L0_attn_Wq, L0_attn_bq, L0_attn_Wk, L0_attn_bk, L0_attn_Wv, L0_attn_bv, L0_attn_Wl, L0_attn_bl, L0_attn_Wo, L0_attn_bo, L0_ffn_gate_w, L0_ffn_gate_b, L0_ffn_w1, L0_ffn_b1, L0_ffn_w2, L0_ffn_b2, L0_ffn_ln_g, L0_ffn_ln_b):

    def _L0_attn_ref(x, Wq, bq, Wk, bk, Wv, bv, Wl, bl, Wo, bo):
        import math
        import jax, jax.numpy as jnp
        import numpy as np
        B, T, E, H, L = (2, 256, 128, 16, 128)
        b, t, e = x.shape
        hd = e // H
        lhd = L // H
        scale = 1.0 / math.sqrt(hd)
        q = (x @ Wq + bq).reshape(b, t, H, hd).transpose(0, 2, 1, 3)
        k = ((x @ Wk + bk) @ Wl + bl).reshape(b, t, H, lhd).transpose(0, 2, 1, 3)
        v = ((x @ Wv + bv) @ Wl + bl).reshape(b, t, H, lhd).transpose(0, 2, 1, 3)
        attn = jax.nn.softmax(jnp.einsum('bhqd,bhkd->bhqk', q, k) * scale, axis=-1)
        out = jnp.einsum('bhqk,bhkd->bhqd', attn, v)
        out = out.transpose(0, 2, 1, 3).reshape(b, t, L)
        return out @ Wo + bo

    def _L0_ffn_ref(x, gate_w, gate_b, w1, b1, w2, b2, ln_g, ln_b):
        import jax, jax.numpy as jnp
        import numpy as np
        TOP_K = 2
        TEMP = 0.9
        EPS = 1e-05
        B, S, D, F, E = (2, 256, 128, 512, 8)

        def _moe_forward(x, gate_w, gate_b, w1, b1, w2, b2, ln_g, ln_b):
            logits = (x @ gate_w + gate_b) / TEMP
            topk_vals, topk_idx = jax.lax.top_k(logits, TOP_K)
            keep = jax.nn.one_hot(topk_idx, E, dtype=jnp.bool_).any(-2)
            masked = jnp.where(keep, logits, -jnp.inf)
            gate_probs = jax.nn.softmax(masked, axis=-1)
            h = jnp.einsum('bsd,edf->bsef', x, w1) + b1
            h = jax.nn.gelu(h, approximate=False)
            expert_out = jnp.einsum('bsef,efd->bsed', h, w2) + b2
            out = jnp.einsum('bse,bsed->bsd', gate_probs, expert_out)
            mu = out.mean(-1, keepdims=True)
            var = out.var(-1, keepdims=True)
            out = (out - mu) / jnp.sqrt(var + EPS) * ln_g + ln_b
            return out
        return _moe_forward(x, gate_w, gate_b, w1, b1, w2, b2, ln_g, ln_b)
    x = L0_attn_x
    xn = _layernorm(x, axis=-1)
    x = x + _L0_attn_ref(xn, L0_attn_Wq, L0_attn_bq, L0_attn_Wk, L0_attn_bk, L0_attn_Wv, L0_attn_bv, L0_attn_Wl, L0_attn_bl, L0_attn_Wo, L0_attn_bo) + _L0_ffn_ref(xn, L0_ffn_gate_w, L0_ffn_gate_b, L0_ffn_w1, L0_ffn_b1, L0_ffn_w2, L0_ffn_b2, L0_ffn_ln_g, L0_ffn_ln_b)
    return x

_drawn_inputs = setup_inputs


def setup_inputs(seed=0):
    import zlib

    import numpy as np

    out = dict(_drawn_inputs(seed))
    spreads = {'L0_attn_bq': (0.0, 0.8),
     'L0_attn_bk': (0.0, 0.8),
     'L0_attn_bv': (0.0, 0.8),
     'L0_attn_bl': (0.0, 0.552),
     'L0_attn_bo': (0.0, 0.1),
     'L0_ffn_gate_b': (0.0, 0.1),
     'L0_ffn_b1': (0.0, 0.1),
     'L0_ffn_b2': (0.0, 0.1),
     'L0_ffn_ln_g': (1.0, 0.2),
     'L0_ffn_ln_b': (0.0, 0.1)}
    factors = {'L0_attn_Wq': 8.0,
     'L0_attn_Wk': 8.0,
     'L0_attn_Wv': 8.0,
     'L0_attn_Wl': 8.0,
     'L0_attn_Wo': 3.571}
    for name, (base, spread) in spreads.items():
        noise = np.random.default_rng([zlib.crc32(name.encode()), seed]).standard_normal(out[name].shape)
        drawn = base * np.exp(spread * noise) if base else spread * noise
        out[name] = jnp.asarray(drawn.astype(out[name].dtype))
    for name, factor in factors.items():
        out[name] = (out[name] * factor).astype(out[name].dtype)
    return out
```

```python
from contextlib import ExitStack

import numpy as np

import concourse.bass as bass
from concourse import mybir
from concourse.alu_op_type import AluOpType as ALU

F32 = mybir.dt.float32
F32R = mybir.dt.float32r
ACT = mybir.ActivationFunctionType
AX = mybir.AxisListType

P = 128
D = 128
SEQ = 256
BLK = 512
T = BLK // P
H = 16
HD = D // H
PL = H // 4
E = 8
FF = 512
FC = FF // P
NCH = E * FC
EPS = 1e-5
TEMP = 0.9
SCALE = 1.0 / float(np.sqrt(HD))

RING = 10
HRING = 4
LAG = 8
DVE_CHUNKS = (0, 2, 4, 6)
PSLOTS = 2
UNITS = H
MAX0 = 10
NORM_AT = 6
WO_AT = 10
MT_AT = 28
STAGE = 6
DOWN_AT = (-1, -1, -1, 0, 1, 2, 3, 4)
GT_AT = 1
ACCT_AT = 6
XT_AT = 8
QK_AT = 11
UP0_AT = 13


def build(nc, x, wq, bq, wk, bk, wv, bv, wl, wlp, bl, blp, wo, bo, gate_w, gate_b, w1, b1t, w2, b2t,
          ln_g, ln_b, out):
    NB = x.shape[0] * x.shape[1] // BLK
    x_blk = x.rearrange("(b s) (p u) d -> b p s (u d)", s=2, u=2)
    out_blk = out.rearrange("(b s) (p u) d -> b p s (u d)", s=2, u=2)

    with ExitStack() as ctx:
        def sb(name, shape, dt=F32):
            return ctx.enter_context(nc.sbuf_tensor(name, shape, dt))

        def ps(name, shape):
            return ctx.enter_context(nc.psum_tensor(name, shape, F32))

        def sem(name):
            return ctx.enter_context(nc.semaphore(name))

        q_dram = nc.dram_tensor("q_dram", [4, 32, PL, BLK], F32).ap()
        k_dram = nc.dram_tensor("k_dram", [4, 32, PL, BLK], F32).ap()
        m_dram = nc.dram_tensor("m_dram", [4, PL, BLK], F32).ap()
        g_dram = nc.dram_tensor("g_dram", [E, BLK], F32).ap()
        o_dram = nc.dram_tensor("o_dram", [4, 32, PL, BLK], F32).ap()

        w1_hi, w1_lo = sb("w1_hi", [P, NCH, P], F32R), sb("w1_lo", [P, NCH, P], F32R)
        w2_hi, w2_lo = sb("w2_hi", [P, NCH, P], F32R), sb("w2_lo", [P, NCH, P], F32R)
        wq_hi, wq_lo = sb("wq_hi", [P, D], F32R), sb("wq_lo", [P, D], F32R)
        wk_hi, wk_lo = sb("wk_hi", [P, D], F32R), sb("wk_lo", [P, D], F32R)
        wv_hi, wv_lo = sb("wv_hi", [P, D], F32R), sb("wv_lo", [P, D], F32R)
        gw_hi, gw_lo = sb("gw_hi", [P, E], F32R), sb("gw_lo", [P, E], F32R)
        wo_sb = sb("wo_sb", [P, D])
        cols = sb("cols", [P, 4])
        bv_col = sb("bv_col", [P, 1])
        b1_sb = sb("b1_sb", [P, NCH])
        b2_sb = sb("b2_sb", [P, E])
        gb_bc = sb("gb_bc", [P, E])
        v_bias = sb("v_bias", [P, D])
        res_bias = sb("res_bias", [P, D])
        lng_bc = sb("lng_bc", [P, D])
        ident = sb("ident", [P, P])
        gw_raw = sb("gw_raw", [P, E])
        before = sb("before", [P, E, E])
        pause = sb("pause", [P, 1])
        half = sb("half", [P, T])

        x_sb = sb("x_sb", [P, T, D])
        stats, mv, vare, rstd = sb("stats", [P, T, 6]), sb("mv", [P, T, 2]), sb("vare", [P, T]), sb("rstd", [P, T])
        xn = sb("xn", [P, T, D])
        xT_next = sb("xT_next", [P, 2, BLK], F32R)
        xT = sb("xT", [P, 2, BLK], F32R)
        Qs, Ks = sb("Qs", [P, PL, BLK], F32R), sb("Ks", [P, PL, BLK], F32R)
        V1 = sb("V1", [P, T, H, 2 * HD])
        mx = sb("mx", [P, T, H])
        mT = sb("mT", [H, BLK], F32R)
        prob = sb("prob", [P, PSLOTS, 2, BLK])
        o_sb = sb("o_sb", [P, PL, BLK])
        num, den = sb("num", [P, BLK]), sb("den", [P, BLK])
        xres, base = sb("xres", [P, T, D]), sb("base", [P, T, D])
        z, gexp, gate = sb("z", [P, T, E]), sb("gexp", [P, T, E]), sb("gate", [P, T, E])
        keep, gmax, gsum = sb("keep", [P, T, E]), sb("gmax", [P, T]), sb("gsum", [P, T])
        cmp_a, cmp_b = sb("cmp_a", [P, T, E, E]), sb("cmp_b", [P, T, E, E])
        gT = sb("gT", [E, BLK])
        G = sb("G", [P, E, BLK])
        h = sb("h", [P, HRING, BLK])
        h_hi, h_lo = sb("h_hi", [P, RING, BLK], F32R), sb("h_lo", [P, RING, BLK], F32R)
        q_hl, k_hl = h_hi[:, STAGE:STAGE + 2, :], h_hi[:, STAGE + 2:STAGE + 4, :]
        y_g, accT = sb("y_g", [P, BLK]), sb("accT", [P, BLK])
        stats2, mv2, vare2, rstd2 = sb("stats2", [P, T, 6]), sb("mv2", [P, T, 2]), sb("vare2", [P, T]), sb("rstd2", [P, T])
        fin = sb("fin", [P, T, D])

        up_ps = ps("up_ps", [P, 2, BLK])
        y_ps = ps("y_ps", [P, 2, BLK])
        s_ps = ps("s_ps", [P, 2, 2, BLK])
        a_ps, b_ps = y_ps[:, 0, :], y_ps[:, 1, :]
        mT_ps = s_ps[0:H, 0, 0, :]

        w_in = sem("w_in")
        stage_in = [sem("stage_in0"), sem("stage_in1")]
        stage_used = sem("stage_used")
        small_ready = sem("small_ready")
        const_ready = sem("const_ready")
        dve_const = sem("dve_const")
        w_hi_done = sem("w_hi_done")
        setup_pe = sem("setup_pe")
        x_in = sem("x_in")
        ln1_step = sem("ln1_step")
        rstd_ready = sem("rstd_ready")
        xn_ready = sem("xn_ready")
        xres_ready = sem("xres_ready")
        xT_ps_ready = sem("xT_ps_ready")
        xT_step = sem("xT_step")
        qkvg_ps = sem("qkvg_ps")
        strips_set = sem("strips_set")
        strips_stored = sem("strips_stored")
        qk_split = sem("qk_split")
        v_ready = sem("v_ready")
        z_step = sem("z_step")
        keep_step = sem("keep_step")
        qk_stored = sem("qk_stored")
        qk_loaded = [sem("qk_loaded0"), sem("qk_loaded1")]
        scores_ready = sem("scores_ready")
        max_done = sem("max_done")
        mT_ps_ready = sem("mT_ps_ready")
        mT_ready = sem("mT_ready")
        m_stored = sem("m_stored")
        m_loaded = sem("m_loaded")
        exp_done = sem("exp_done")
        av_done = sem("av_done")
        o_out = sem("o_out")
        o_stored = sem("o_stored")
        o_loaded = sem("o_loaded")
        norm_step = sem("norm_step")
        wo_ps_ready = sem("wo_ps_ready")
        base_ready = sem("base_ready")
        gexp_ready = sem("gexp_ready")
        gate_step = sem("gate_step")
        gT_ps_ready = sem("gT_ps_ready")
        gT_ready = sem("gT_ready")
        g_stored = sem("g_stored")
        g_loaded = sem("g_loaded")
        xT_moved = sem("xT_moved")
        up_done = sem("up_done")
        gelu_done = sem("gelu_done")
        lo_done = sem("lo_done")
        split_step = sem("split_step")
        down_done = sem("down_done")
        acc_step = sem("acc_step")
        accT_ps_ready = sem("accT_ps_ready")
        ln2_step = sem("ln2_step")
        rstd2_ready = sem("rstd2_ready")
        fin_step = sem("fin_step")
        out_done = sem("out_done")

        W_SMALL = 16 * 18
        LN1, LN2, ZST, KEEP, GST, NORM = 3, 4, 3, 6, 4, 2
        ACC = 2 * E

        def unit(n):
            return n // 4, n % 2 * 2, n // 2 % 2

        def gelus(b, n):
            return b * (2 * NCH - len(DVE_CHUNKS)) + 2 * (n + 1) - sum(m <= n for m in DVE_CHUNKS)

        def lows(b, n):
            return b * (NCH - len(DVE_CHUNKS)) + n + 1 - sum(m <= n for m in DVE_CHUNKS)

        def split_of(b, n):
            if n in DVE_CHUNKS:
                return split_step, b * 2 * len(DVE_CHUNKS) + 2 * DVE_CHUNKS.index(n) + 2
            return lo_done, lows(b, n)

        def has_max_unit(n):
            return MAX0 <= n < MAX0 + UNITS

        w1_v = w1.rearrange("e d f -> d e f")
        w2_v = w2.rearrange("e (c p) d -> p (e c) d", p=P)
        halves = [w1_v[:, 0:4, :], w1_v[:, 4:8, :], w2_v[:, 0:16, :], w2_v[:, 16:32, :]]

        block = ctx.enter_context(nc.Block())

        @block.sync
        def _(sp):
            sp.dma_start(x_sb[:, :, :].rearrange("p (s u) d -> p s (u d)", s=2), x_blk[0]).then_inc(x_in, 16)
            for dst, src in ((cols[:, 0:1], bq), (cols[:, 1:2], bk), (cols[:, 2:3], blp), (bv_col[:, :], bv),
                             (xn[:, 0, :], wq), (xn[:, 1, :], wk), (xn[:, 2, :], wv), (xn[:, 3, :], wl),
                             (xres[:, 0, :], wlp)):
                sp.dma_start(dst, src).then_inc(w_in, 16)
            for n in range(2):
                sp.dma_start(G[:, 4 * n:4 * n + 4, :], halves[n]).then_inc(stage_in[n], 16)

            def store_qk():
                for dram, t, src in ((q_dram, q_hl, (0, 0, 1)), (k_dram, k_hl, (0, 1, 0))):
                    for c in range(3):
                        sp.dma_start(dram[:, 8 * c:8 * c + 8, :, :].rearrange("j r g n -> (r g) j n"),
                                     t[:, src[c], :].bitcast(F32)).then_inc(qk_stored, 16)

            def load_qk():
                for side, planes in enumerate((slice(0, PL // 2), slice(PL // 2, PL))):
                    for strips, dram in ((Qs, q_dram), (Ks, k_dram)):
                        sp.dma_start(strips[:, planes, :].bitcast(F32),
                                     dram[:, :, planes, :].rearrange("j r g n -> (j r) g n")).then_inc(qk_loaded[side], 16)

            def store_o(planes):
                sp.dma_start(o_dram[:, :, planes, :].rearrange("j r g n -> (j r) g n"), o_sb[:, planes, :]).then_inc(o_stored, 16)

            def block_moves(b, x_next, first=False, last=False):
                s = (lambda v: v) if isinstance(b, int) else sp.snap
                w_split, w_qks, w_max = s(b * 4 + 8), s(b * 96 + 192), s(b + 1)
                w_16, w_scores = s(b * 16 + 16), s(b * 2 * UNITS + 2 * UNITS)
                w_ohalf, w_olast, w_o2 = s(b * 4 + 2), s(b * 4 + 4), s(b * 32 + 32)
                w_acc, w_up, w_xt = s(b * ACC), s(b * NCH), s(b * 2 + 2)
                sp.wait_ge(mT_ready, w_max)
                sp.dma_start(m_dram.rearrange("j g n -> (j g) n"), mT[:, :].bitcast(F32)).then_inc(m_stored, 16)
                sp.wait_ge(m_stored, w_16)
                sp.dma_start(Qs[24:P:32, :, :].bitcast(F32), m_dram).then_inc(m_loaded, 16)
                sp.wait_ge(xn_ready, w_max)
                sp.wait_ge(xres_ready, w_max)
                sp.dma_start(x_sb[:, :, :].rearrange("p (s u) d -> p s (u d)", s=2), x_next).then_inc(x_in, 16)
                if not first:
                    sp.wait_ge(up_done, w_up)
                else:
                    sp.wait_ge(xT_step, w_xt)
                sp.dma_start(xT[:, :, :].bitcast(F32), xT_next[:, :, :].bitcast(F32)).then_inc(xT_moved, 16)
                sp.wait_ge(gT_ready, w_max)
                sp.dma_start(g_dram, gT[:, :]).then_inc(g_stored, 16)
                sp.wait_ge(g_stored, w_16)
                if not first:
                    sp.wait_ge(acc_step, w_acc)
                else:
                    sp.wait_ge(stage_used, 4)
                sp.dma_start(G[:, :, :], g_dram.partition_broadcast(P)).then_inc(g_loaded, 16)
                sp.wait_ge(o_out, w_ohalf)
                store_o(slice(0, PL // 2))
                if not last:
                    sp.wait_ge(qk_split, w_split)
                    store_qk()
                sp.wait_ge(o_out, w_olast)
                store_o(slice(PL // 2, PL))
                sp.wait_ge(o_stored, w_o2)
                sp.dma_start(num[:, :], o_dram[:, 0:8, :, :].rearrange("j r g n -> (r g) j n")).then_inc(o_loaded, 16)
                sp.dma_start(den[:, :], o_dram[:, 8:16, :, :].rearrange("j r g n -> (r g) j n")).then_inc(o_loaded, 16)
                if not last:
                    sp.wait_ge(qk_stored, w_qks)
                    sp.wait_ge(scores_ready, w_scores)
                    load_qk()

            sp.wait_ge(qk_split, 4)
            store_qk()
            sp.wait_ge(qk_stored, 96)
            sp.wait_ge(strips_stored, 128)
            load_qk()
            block_moves(0, x_blk[1], first=True)
            with sp.Fori(0, NB - 2) as i:
                block_moves(i + 1, x_blk[2:NB][i])
            block_moves(NB - 1, x_blk[NB - 1], last=True)

        @block.gpsimd
        def _(pool):
            nc.gpsimd.memset(ident[:, :], 0.0)
            nc.gpsimd.memset(before[:, :, :], 1.0)
            nc.gpsimd.memset(half[:, :], -0.5).then_inc(const_ready, 1)
            pool.wait_ge(const_ready, 1)
            nc.gpsimd.affine_select(out=ident[:, :], in_=ident[:, :], compare_op=ALU.not_equal, fill=1.0,
                                    base=0, pattern=[[-1, P]], channel_multiplier=1).then_inc(const_ready, 1)
            nc.gpsimd.affine_select(out=before[:, :, :], in_=before[:, :, :], compare_op=ALU.is_gt, fill=0.0,
                                    base=0, pattern=[[1, E], [-1, E]], channel_multiplier=0).then_inc(const_ready, 1)
            pool.wait_ge(const_ready, 3)

            def rstd_of(b):
                pool.wait_ge(ln1_step, b * LN1 + 3)
                nc.gpsimd.tensor_tensor(rstd[:, :], vare[:, :], half[:, :], ALU.pow).then_inc(rstd_ready, 1)

            def residual(b, first):
                if not first:
                    pool.wait_ge(base_ready, b)
                pool.wait_ge(x_in, b * 16 + 16)
                nc.gpsimd.tensor_tensor(xres[:, :, :], x_sb[:, :, :], res_bias[:, :].unsqueeze(1).broadcast_to((P, T, D)),
                                        ALU.add).then_inc(xres_ready, 1)

            def low_part(b, n):
                pool.wait_ge(gelu_done, gelus(b, n))
                if n >= RING:
                    pool.wait_ge(down_done, b * NCH + n - RING + 1)
                nc.gpsimd.tensor_tensor(h_lo[:, n % RING, :], h[:, n % HRING, :], h_hi[:, n % RING, :].bitcast(F32),
                                        ALU.subtract).then_inc(lo_done, 1)

            def rstd2_of(b):
                pool.wait_ge(ln2_step, b * LN2 + 3)
                nc.gpsimd.tensor_tensor(rstd2[:, :], vare2[:, :], half[:, :], ALU.pow).then_inc(rstd2_ready, 1)

            def result(b):
                pool.wait_ge(ln2_step, b * LN2 + 4)
                nc.gpsimd.tensor_tensor(fin[:, :, :], fin[:, :, :], lng_bc[:, :].unsqueeze(1).broadcast_to((P, T, D)),
                                        ALU.mult).then_inc(fin_step, 1)
                pool.wait_ge(fin_step, b * 2 + 1)
                nc.gpsimd.tensor_tensor(fin[:, :, :], fin[:, :, :], base[:, :, :], ALU.add).then_inc(fin_step, 1)

            def split_w(n):
                stage = G[:, 4 * (n % 2):4 * (n % 2) + 4, :].rearrange("p a (b c) -> p (a b) c", c=P)
                hi, lo = ((w1_hi, w1_lo), (w2_hi, w2_lo))[n // 2]
                at = slice(16 * (n % 2), 16 * (n % 2) + 16)
                pool.wait_ge(stage_in[n % 2], 16 * (n // 2) + 16)
                nc.gpsimd.tensor_copy(hi[:, at, :], stage).then_inc(w_hi_done, 1)
                pool.wait_ge(w_hi_done, n + 1)
                nc.gpsimd.tensor_tensor(lo[:, at, :], stage, hi[:, at, :].bitcast(F32), ALU.subtract).then_inc(stage_used, 1)

            pool.sem_inc(out_done, 16)
            rstd_of(0)
            pool.wait_ge(small_ready, 1)
            residual(0, True)
            for n in range(4):
                split_w(n)
            rstd_of(1)
            with pool.Fori(0, NB - 1) as i:
                for n in range(NCH):
                    if n not in DVE_CHUNKS:
                        low_part(i, n)
                    if n == WO_AT + 1:
                        residual(i + 1, False)
                rstd_of(i + 2)
                rstd2_of(i)
                result(i)
            for n in range(NCH):
                if n not in DVE_CHUNKS:
                    low_part(NB - 1, n)
            rstd2_of(NB - 1)
            result(NB - 1)

        @block.scalar
        def _(act):
            for dst, src in ((wo_sb[:, :], wo), (gw_raw[:, :], gate_w), (b1_sb[:, :], b1t),
                             (b2_sb[:, :], b2t), (gb_bc[:, :], gate_b.partition_broadcast(P)),
                             (xres[:, 1, :], bl.partition_broadcast(P)), (res_bias[:, :], bo.partition_broadcast(P)),
                             (xres[:, 2, :], ln_b.partition_broadcast(P)), (lng_bc[:, :], ln_g.partition_broadcast(P))):
                act.dma_start(dst, src).then_inc(w_in, 16)
            act.wait_ge(strips_set, 1)
            for dram in (q_dram, k_dram):
                for j in range(4):
                    act.dma_start(dram[j, 24:32], Ks[0:8, :, :].bitcast(F32)).then_inc(strips_stored, 16)
            act.wait_ge(small_ready, 1)

            def gate_exp(b):
                act.wait_ge(z_step, b * ZST + 2)
                nc.scalar.activation(gexp[:, :, :], z[:, :, :], ACT.Exp, scale=1.0 / TEMP).then_inc(gexp_ready, 1)

            def softmax_exp(b, n):
                act.wait_ge(scores_ready, b * 2 * UNITS + UNITS + n + 1)
                if n >= PSLOTS:
                    act.wait_ge(av_done, b * UNITS + n - PSLOTS + 1)
                nc.scalar.activation(prob[:, n % PSLOTS], s_ps[:, n % 2], ACT.Exp, scale=SCALE).then_inc(exp_done, 1)

            def gelu(b, n, stage_free):
                act.wait_ge(up_done, b * NCH + n + 1)
                if n >= HRING:
                    act.wait_ge(*split_of(b, n - HRING))
                nc.scalar.activation(h[:, n % HRING, :], up_ps[:, n % 2, :], ACT.Gelu, bias=b1_sb[:, n:n + 1]).then_inc(gelu_done, 1)
                if n in DVE_CHUNKS:
                    return
                if n == STAGE + 1:
                    act.wait_ge(*stage_free)
                if n >= RING:
                    act.wait_ge(down_done, b * NCH + n - RING + 1)
                nc.scalar.activation(h_hi[:, n % RING, :], up_ps[:, n % 2, :], ACT.Gelu, bias=b1_sb[:, n:n + 1]).then_inc(gelu_done, 1)

            def softmax_phase(b):
                gate_exp(b)
                for n in range(UNITS):
                    softmax_exp(b, n)

            def store_out(b):
                act.wait_ge(fin_step, b * 2 + 2)
                act.dma_start(out_blk[b], fin[:, :, :].rearrange("p (s u) d -> p s (u d)", s=2)).then_inc(out_done, 16)

            for n in range(2):
                act.wait_ge(stage_used, n + 1)
                act.dma_start(G[:, 4 * n:4 * n + 4, :].rearrange("p a (b c) -> p (a b) c", c=P),
                              halves[2 + n]).then_inc(stage_in[n], 16)
            softmax_phase(0)
            with act.Fori(0, NB - 1) as i:
                for n in range(NCH):
                    gelu(i, n, (qk_stored, i * 96 + 192))
                softmax_phase(i + 1)
                store_out(i)
            for n in range(NCH):
                gelu(NB - 1, n, (qk_split, NB * 4 + 4))
            store_out(NB - 1)
            act.wait_ge(out_done, 16 * NB + 16)

        @block.vector
        def _(dve):
            def setup():
                count = [0]

                def step(ins):
                    count[0] += 1
                    ins.then_inc(dve_const, 1)

                def stepped():
                    dve.wait_ge(dve_const, count[0])

                nc.vector.memset(Ks[:, :, :].bitcast(F32), -1.0).then_inc(strips_set, 1)
                nc.vector.memset(up_ps[:, :, :], 0.0)
                step(nc.vector.memset(V1[:, :, :, HD:2 * HD], 1.0))
                dve.wait_ge(w_in, W_SMALL)
                step(nc.vector.tensor_copy(base[:, 0, :], bv_col[:, :].broadcast_to((P, D))))
                assert count[0] == 2
                nc.vector.tensor_copy(wq_hi[:, :], xn[:, 0, :])
                step(nc.vector.tensor_copy(gw_hi[:, :], gw_raw[:, :]))
                stepped()
                nc.vector.tensor_tensor(wq_lo[:, :], xn[:, 0, :], wq_hi[:, :].bitcast(F32), ALU.subtract)
                nc.vector.tensor_tensor(gw_lo[:, :], gw_raw[:, :], gw_hi[:, :].bitcast(F32), ALU.subtract)
                nc.vector.tensor_tensor(res_bias[:, :], res_bias[:, :], xres[:, 2, :], ALU.add)
                dve.wait_ge(setup_pe, 1)
                nc.vector.tensor_copy(base[:, 1:3, :], a_ps[:, 0:2 * D].rearrange("p (a b) -> p a b", a=2)).then_inc(dve_const, 1)
                count[0] += 1
                assert count[0] == 4
                dve.wait_ge(setup_pe, 2)
                nc.vector.tensor_copy(wk_hi[:, :], b_ps[:, 0:D])
                step(nc.vector.tensor_copy(wv_hi[:, :], b_ps[:, D:2 * D]))
                stepped()
                nc.vector.tensor_tensor(wk_lo[:, :], b_ps[:, 0:D], wk_hi[:, :].bitcast(F32), ALU.subtract)
                nc.vector.tensor_tensor(wv_lo[:, :], b_ps[:, D:2 * D], wv_hi[:, :].bitcast(F32), ALU.subtract)
                nc.vector.tensor_tensor(v_bias[:, :], b_ps[:, 2 * D:3 * D], xres[:, 1, :], ALU.add)
                nc.vector.tensor_tensor(cols[:, 3:4], b_ps[:, 3 * D:3 * D + 1], cols[:, 2:3], ALU.add).then_inc(small_ready, 1)
                dve.wait_ge(small_ready, 1)

            def norm_stats(b, src, st, agg, ve, steps, per):
                for t in range(T):
                    last = nc.vector.bn_stats(st[:, t, :], src(t))
                last.then_inc(steps, 1)
                dve.wait_ge(steps, b * per + 1)
                nc.vector.memset(pause[:, :], 0.0)
                for t in range(T):
                    last = nc.vector.bn_aggr(agg[:, t, :], st[:, t, :])
                last.then_inc(steps, 1)
                dve.wait_ge(steps, b * per + 2)
                nc.vector.tensor_scalar(ve[:, :], agg[:, :, 1], EPS, None, ALU.add).then_inc(steps, 1)

            def ln1_stats(b):
                dve.wait_ge(x_in, b * 16 + 16)
                norm_stats(b, lambda t: x_sb[:, t, :], stats, mv, vare, ln1_step, LN1)

            def ln1_apply(b):
                dve.wait_ge(rstd_ready, b + 1)
                for t in range(T):
                    last = nc.vector.tensor_scalar(xn[:, t, :], x_sb[:, t, :], mv[:, t, 0:1], rstd[:, t:t + 1],
                                                   ALU.subtract, ALU.mult)
                last.then_inc(xn_ready, 1)

            def take_xT(b, first):
                dve.wait_ge(xT_ps_ready, b + 1)
                if not first:
                    dve.wait_ge(xT_moved, b * 16)
                nc.vector.tensor_copy(xT_next[:, 0, :], b_ps).then_inc(xT_step, 1)
                dve.wait_ge(xT_step, b * 2 + 1)
                nc.vector.tensor_tensor(xT_next[:, 1, :], b_ps, xT_next[:, 0, :].bitcast(F32),
                                        ALU.subtract).then_inc(xT_step, 1)

            def split_qk(b):
                for m, (ps_, bias, hl) in enumerate(((a_ps, cols[:, 0:1], q_hl), (b_ps, cols[:, 3:4], k_hl))):
                    dve.wait_ge(qkvg_ps, b * 4 + m + 1)
                    nc.vector.tensor_scalar(hl[:, 0, :], ps_, bias, None, ALU.add).then_inc(qk_split, 1)
                    dve.wait_ge(qk_split, b * 4 + 2 * m + 1)
                    nc.vector.scalar_tensor_tensor(hl[:, 1, :], ps_, bias, hl[:, 0, :].bitcast(F32), ALU.add,
                                                   ALU.subtract).then_inc(qk_split, 1)

            def take_v(b, first):
                dve.wait_ge(qkvg_ps, b * 4 + 3)
                nc.vector.tensor_tensor(V1[:, :, :, 0:HD], a_ps.rearrange("p (t h d) -> p t h d", t=T, h=H),
                                        v_bias[:, :].rearrange("p (h d) -> p h d", h=H).unsqueeze(1).broadcast_to((P, T, H, HD)),
                                        ALU.add).then_inc(v_ready, 1)

            def take_logits(b):
                dve.wait_ge(qkvg_ps, b * 4 + 4)
                nc.vector.tensor_tensor(z[:, :, :], b_ps[:, 0:T * E].rearrange("p (t e) -> p t e", t=T),
                                        gb_bc[:, :].unsqueeze(1).broadcast_to((P, T, E)), ALU.add).then_inc(z_step, 1)
                dve.wait_ge(z_step, b * ZST + 1)
                nc.vector.tensor_reduce(gmax[:, :], z[:, :, :], axis=AX.X, op=ALU.max).then_inc(keep_step, 1)
                mine = z[:, :, :].unsqueeze(3).broadcast_to((P, T, E, E))
                other = z[:, :, :].unsqueeze(2).broadcast_to((P, T, E, E))
                nc.vector.tensor_tensor(cmp_a[:, :, :, :], other, mine, ALU.is_equal).then_inc(keep_step, 1)
                nc.vector.tensor_tensor(cmp_b[:, :, :, :], other, mine, ALU.is_gt).then_inc(keep_step, 1)
                dve.wait_ge(keep_step, b * KEEP + 2)
                nc.vector.tensor_tensor(cmp_a[:, :, :, :].rearrange("p t e f -> p t (e f)"),
                                        cmp_a[:, :, :, :].rearrange("p t e f -> p t (e f)"),
                                        before[:, :, :].rearrange("p e f -> p (e f)").unsqueeze(1).broadcast_to((P, T, E * E)),
                                        ALU.mult).then_inc(keep_step, 1)
                dve.wait_ge(keep_step, b * KEEP + 4)
                nc.vector.tensor_tensor(cmp_a[:, :, :, :], cmp_a[:, :, :, :], cmp_b[:, :, :, :], ALU.add).then_inc(keep_step, 1)
                dve.wait_ge(keep_step, b * KEEP + 5)
                nc.vector.tensor_reduce(keep[:, :, :], cmp_a[:, :, :, :], axis=AX.X, op=ALU.add).then_inc(keep_step, 1)
                nc.vector.tensor_tensor(z[:, :, :], z[:, :, :], gmax[:, :].unsqueeze(2).broadcast_to((P, T, E)),
                                        ALU.subtract).then_inc(z_step, 1)
                dve.wait_ge(keep_step, b * KEEP + 6)
                nc.vector.tensor_scalar(keep[:, :, :], keep[:, :, :], 1.5, None, ALU.is_lt).then_inc(z_step, 1)

            def take_max(b, n):
                g, j, s = unit(n)
                dve.wait_ge(scores_ready, b * 2 * UNITS + n + 1)
                heads = slice(4 * j + g, 4 * j + g + 5, 4)
                nc.vector.tensor_reduce(mx[:, 2 * s:2 * s + 2, heads].rearrange("p u j -> p j u"),
                                        s_ps[:, n % 2].rearrange("p j (u k) -> p j u k", u=2),
                                        axis=AX.X, op=ALU.max).then_inc(max_done, 1)

            def take_mT(b, first):
                dve.wait_ge(mT_ps_ready, b + 1)
                if not first:
                    dve.wait_ge(m_stored, b * 16)
                nc.vector.tensor_copy(mT[:, :], mT_ps).then_inc(mT_ready, 1)

            def gates(b):
                dve.wait_ge(gexp_ready, b + 1)
                nc.vector.tensor_tensor(gexp[:, :, :], gexp[:, :, :], keep[:, :, :], ALU.mult).then_inc(gate_step, 1)
                dve.wait_ge(gate_step, b * GST + 1)
                nc.vector.tensor_reduce(gsum[:, :], gexp[:, :, :], axis=AX.X, op=ALU.add).then_inc(gate_step, 1)
                dve.wait_ge(gate_step, b * GST + 2)
                nc.vector.reciprocal(gsum[:, :], gsum[:, :]).then_inc(gate_step, 1)
                dve.wait_ge(gate_step, b * GST + 3)
                nc.vector.tensor_tensor(gate[:, :, :], gexp[:, :, :], gsum[:, :].unsqueeze(2).broadcast_to((P, T, E)),
                                        ALU.mult).then_inc(gate_step, 1)

            def take_gT(b, first):
                dve.wait_ge(gT_ps_ready, b + 1)
                if not first:
                    dve.wait_ge(g_stored, b * 16)
                nc.vector.tensor_copy(gT[:, :], up_ps[0:E, 1, :]).then_inc(gT_ready, 1)

            def take_o(b, g, first):
                dve.wait_ge(av_done, b * UNITS + 4 * g + 4)
                if g == 0 and not first:
                    dve.wait_ge(o_stored, b * 32)
                nc.vector.tensor_copy(o_sb[:, g, :], up_ps[:, g % 2, :]).then_inc(o_out, 1)

            def attn_norm(b):
                dve.wait_ge(o_loaded, b * 32 + 32)
                nc.vector.reciprocal(den[:, :], den[:, :]).then_inc(norm_step, 1)
                dve.wait_ge(norm_step, b * NORM + 1)
                nc.vector.tensor_tensor(num[:, :], num[:, :], den[:, :], ALU.mult).then_inc(norm_step, 1)

            def attn_add(b):
                dve.wait_ge(wo_ps_ready, b + 1)
                dve.wait_ge(xres_ready, b + 1)
                dve.wait_ge(lo_done, lows(b, 1))
                nc.vector.tensor_tensor(base[:, :, :], b_ps.rearrange("p (t d) -> p t d", t=T), xres[:, :, :],
                                        ALU.add).then_inc(base_ready, 1)

            def split_h(b, n, stage_free):
                if n == STAGE:
                    dve.wait_ge(*stage_free)
                dve.wait_ge(gelu_done, gelus(b, n))
                nc.vector.tensor_copy(h_hi[:, n % RING, :], h[:, n % HRING, :]).then_inc(split_step, 1)
                dve.wait_ge(split_step, split_of(b, n)[1] - 1)
                nc.vector.tensor_tensor(h_lo[:, n % RING, :], h[:, n % HRING, :], h_hi[:, n % RING, :].bitcast(F32),
                                        ALU.subtract).then_inc(split_step, 1)

            def gate_y(b, e):
                if e == 0:
                    dve.wait_ge(g_loaded, b * 16 + 16)
                dve.wait_ge(down_done, b * NCH + FC * (e + 1))
                if e >= 2:
                    dve.wait_ge(acc_step, b * ACC + 2 * e - 1)
                dst = accT[:, :] if e == 0 else y_g[:, :]
                nc.vector.scalar_tensor_tensor(dst, y_ps[:, e % 2, :], b2_sb[:, e:e + 1], G[:, e, :], ALU.add, ALU.mult).then_inc(acc_step, 1)

            def add_y(b, e):
                if e == 0:
                    return
                dve.wait_ge(acc_step, b * ACC + 2 * e)
                nc.vector.tensor_tensor(accT[:, :], accT[:, :], y_g[:, :], ALU.add).then_inc(acc_step, 2 if e == E - 1 else 1)

            def ln2_stats(b):
                dve.wait_ge(accT_ps_ready, b + 1)
                norm_stats(b, lambda t: a_ps[:, t * D:(t + 1) * D], stats2, mv2, vare2, ln2_step, LN2)

            def ln2_apply(b):
                dve.wait_ge(rstd2_ready, b + 1)
                dve.wait_ge(out_done, b * 16 + 16)
                for t in range(T):
                    last = nc.vector.tensor_scalar(fin[:, t, :], a_ps[:, t * D:(t + 1) * D], mv2[:, t, 0:1],
                                                   rstd2[:, t:t + 1], ALU.subtract, ALU.mult)
                last.then_inc(ln2_step, 1)

            ln1_stats(0)
            setup()
            ln1_apply(0)
            take_xT(0, True)
            split_qk(0)
            take_v(0, True)
            take_logits(0)
            for n in range(UNITS):
                take_max(0, n)
            take_mT(0, True)
            gates(0)
            take_gT(0, True)
            ln1_stats(1)
            ln1_apply(1)
            take_o(0, 0, True)
            take_o(0, 1, True)
            take_xT(1, False)
            take_o(0, 2, True)
            split_qk(1)
            take_o(0, 3, True)

            with dve.Fori(0, NB - 1) as i:
                for n in range(NCH):
                    if n == 1:
                        take_v(i + 1, False)
                        take_logits(i + 1)
                    if n in DVE_CHUNKS:
                        split_h(i, n, (qk_stored, i * 96 + 192))
                    if n == NORM_AT:
                        attn_norm(i)
                    if n == WO_AT:
                        attn_add(i)
                    if n > LAG and (n - LAG) % FC == 0:
                        gate_y(i, (n - LAG) // FC - 1)
                    if has_max_unit(n):
                        take_max(i + 1, n - MAX0)
                    if n > LAG and (n - LAG) % FC == 0:
                        add_y(i, (n - LAG) // FC - 1)
                    if n == MT_AT:
                        take_mT(i + 1, False)
                gate_y(i, E - 3)
                add_y(i, E - 3)
                gates(i + 1)
                gate_y(i, E - 2)
                add_y(i, E - 2)
                take_gT(i + 1, False)
                ln1_stats(i + 2)
                take_o(i + 1, 0, False)
                gate_y(i, E - 1)
                add_y(i, E - 1)
                ln1_apply(i + 2)
                ln2_stats(i)
                take_o(i + 1, 1, False)
                ln2_apply(i)
                take_xT(i + 2, False)
                take_o(i + 1, 2, False)
                split_qk(i + 2)
                take_o(i + 1, 3, False)

            last_b = NB - 1
            for n in DVE_CHUNKS:
                split_h(last_b, n, (qk_split, NB * 4 + 4))
            attn_norm(last_b)
            attn_add(last_b)
            for e in range(E):
                gate_y(last_b, e)
                add_y(last_b, e)
            ln2_stats(last_b)
            ln2_apply(last_b)

        @block.tensor
        def _(pe):
            def split_product(dst, w_hi, w_lo, m_hi, m_lo, first=True, last=True):
                nc.tensor.matmul(dst, w_hi, m_hi, start=first, stop=False)
                nc.tensor.matmul(dst, w_lo, m_hi, start=False, stop=False)
                return nc.tensor.matmul(dst, w_hi, m_lo, start=False, stop=last)

            def setup():
                pe.wait_ge(const_ready, 3)
                pe.wait_ge(w_in, W_SMALL)
                nc.tensor.transpose(a_ps[:, 0:D], xn[:, 1, :], ident[:, :])
                nc.tensor.transpose(a_ps[:, D:2 * D], xn[:, 2, :], ident[:, :]).then_inc(setup_pe, 1)
                pe.wait_ge(dve_const, 4)
                nc.tensor.matmul(b_ps[:, 0:D], base[:, 1, :], xres[:, 0, :], start=True, stop=True)
                nc.tensor.matmul(b_ps[:, D:2 * D], base[:, 2, :], xn[:, 3, :], start=True, stop=True)
                nc.tensor.matmul(b_ps[:, 2 * D:3 * D], base[:, 0, :], xn[:, 3, :], start=True, stop=True)
                nc.tensor.matmul(b_ps[:, 3 * D:3 * D + 1], xres[:, 0, :], cols[:, 1:2], start=True, stop=True).then_inc(setup_pe, 1)
                pe.wait_ge(small_ready, 1)

            def make_xT(b, b_ps_used=None):
                if b_ps_used is not None:
                    pe.wait_ge(*b_ps_used)
                pe.wait_ge(xn_ready, b + 1)
                for t in range(T):
                    last = nc.tensor.transpose(b_ps[:, t * P:(t + 1) * P], xn[:, t, :], ident[:, :])
                last.then_inc(xT_ps_ready, 1)

            def make_qk(b, a_ps_used=None):
                pe.wait_ge(xT_step, b * 2 + 2)
                if a_ps_used is not None:
                    pe.wait_ge(*a_ps_used)
                split_product(a_ps, wq_hi[:, :], wq_lo[:, :], xT_next[:, 0, :], xT_next[:, 1, :]).then_inc(qkvg_ps, 1)
                split_product(b_ps, wk_hi[:, :], wk_lo[:, :], xT_next[:, 0, :], xT_next[:, 1, :]).then_inc(qkvg_ps, 1)

            def make_v_logits(b):
                pe.wait_ge(qk_split, b * 4 + 2)
                for t in range(T):
                    tok = slice(t * P, (t + 1) * P)
                    last = split_product(a_ps[:, tok], xT_next[:, 0, tok], xT_next[:, 1, tok], wv_hi[:, :], wv_lo[:, :])
                last.then_inc(qkvg_ps, 1)
                pe.wait_ge(qk_split, b * 4 + 4)
                for t in range(T):
                    tok = slice(t * P, (t + 1) * P)
                    last = split_product(b_ps[:, t * E:(t + 1) * E], xT_next[:, 0, tok], xT_next[:, 1, tok], gw_hi[:, :], gw_lo[:, :])
                last.then_inc(qkvg_ps, 1)

            def max_scores(b, n):
                g, j, s = unit(n)
                if n == 0:
                    pe.wait_ge(qk_loaded[0], b * 32 + 32)
                if n == UNITS // 2:
                    pe.wait_ge(qk_loaded[1], b * 32 + 32)
                if n >= 2:
                    pe.wait_ge(max_done, b * UNITS + n - 1)
                for u in range(2):
                    for d in range(2):
                        rows = slice(32 * (j + d), 32 * (j + d) + 24)
                        last = nc.tensor.matmul(s_ps[:, n % 2, d, u * SEQ:(u + 1) * SEQ],
                                                Qs[rows, g, s * SEQ + u * P:s * SEQ + (u + 1) * P],
                                                Ks[rows, g, s * SEQ:(s + 1) * SEQ], start=True, stop=True)
                last.then_inc(scores_ready, 1)

            def make_mT(b):
                pe.wait_ge(max_done, b * UNITS + UNITS)
                for t in range(T):
                    last = nc.tensor.transpose(mT_ps[:, t * P:(t + 1) * P], mx[:, t, :], ident[:, :])
                last.then_inc(mT_ps_ready, 1)

            def soft_scores(b, n):
                g, j, s = unit(n)
                if n == 0:
                    pe.wait_ge(m_loaded, b * 16 + 16)
                if n >= 2:
                    pe.wait_ge(exp_done, b * UNITS + n - 1)
                for u in range(2):
                    for d in range(2):
                        rows = slice(32 * (j + d), 32 * (j + d) + 25)
                        last = nc.tensor.matmul(s_ps[:, n % 2, d, u * SEQ:(u + 1) * SEQ],
                                                Ks[rows, g, s * SEQ + u * P:s * SEQ + (u + 1) * P],
                                                Qs[rows, g, s * SEQ:(s + 1) * SEQ], start=True, stop=True)
                last.then_inc(scores_ready, 1)

            def weigh(b, n):
                g, j, s = unit(n)
                if n == 4:
                    pe.wait_ge(gT_ready, b + 1)
                if n % 4 == 0 and g >= 2:
                    pe.wait_ge(o_out, b * PL + g - 1)
                pe.wait_ge(exp_done, b * UNITS + n + 1)
                for u in range(2):
                    for d in range(2):
                        rows = slice(32 * (j + d), 32 * (j + d) + 2 * HD)
                        last = nc.tensor.matmul(up_ps[rows, g % 2, s * SEQ:(s + 1) * SEQ], V1[:, 2 * s + u, 4 * (j + d) + g, :],
                                                prob[:, n % PSLOTS, d, u * SEQ:(u + 1) * SEQ], start=u == 0, stop=u == 1)
                last.then_inc(av_done, 1)

            def make_gT(b):
                pe.wait_ge(gate_step, b * GST + 4)
                for t in range(T):
                    last = nc.tensor.transpose(up_ps[0:E, 1, t * P:(t + 1) * P], gate[:, t, :], ident[:, :])
                last.then_inc(gT_ps_ready, 1)

            def attn_out(b, b_ps_used):
                pe.wait_ge(norm_step, b * NORM + 2)
                pe.wait_ge(*b_ps_used)
                for t in range(T):
                    last = nc.tensor.matmul(b_ps[:, t * D:(t + 1) * D], num[:, t * P:(t + 1) * P], wo_sb[:, :],
                                            start=True, stop=True)
                last.then_inc(wo_ps_ready, 1)

            def up(b, n):
                if n == 0:
                    pe.wait_ge(xT_moved, b * 16 + 16)
                if n < 2:
                    pe.wait_ge(o_out, b * PL + PL - 1 + n)
                else:
                    pe.wait_ge(gelu_done, gelus(b, n - 2))
                split_product(up_ps[:, n % 2, :], w1_hi[:, n, :], w1_lo[:, n, :], xT[:, 0, :], xT[:, 1, :]).then_inc(up_done, 1)

            def down(b, n, a_ps_used=None):
                e, c = n // FC, n % FC
                pe.wait_ge(*split_of(b, n))
                if n == 0:
                    pe.wait_ge(*a_ps_used)
                if c == 0 and e == 1:
                    pe.wait_ge(base_ready, b + 1)
                if c == 0 and e >= 2:
                    pe.wait_ge(acc_step, b * ACC + max(1, 2 * (e - 2)))
                split_product(y_ps[:, e % 2, :], w2_hi[:, n, :], w2_lo[:, n, :], h_hi[:, n % RING, :], h_lo[:, n % RING, :],
                              first=c == 0, last=c == FC - 1).then_inc(down_done, 1)

            def make_accT(b):
                pe.wait_ge(acc_step, b * ACC + ACC)
                for t in range(T):
                    last = nc.tensor.transpose(a_ps[:, t * D:(t + 1) * D], accT[:, t * P:(t + 1) * P], ident[:, :])
                last.then_inc(accT_ps_ready, 1)

            def softmax_phase(b, former=None):
                def deferred(n):
                    for m, at in enumerate(DOWN_AT):
                        if at == n and former is not None:
                            down(former, NCH - LAG + m)

                deferred(-1)
                soft_scores(b, 0)
                soft_scores(b, 1)
                for n in range(UNITS):
                    if n + 2 < UNITS:
                        soft_scores(b, n + 2)
                    weigh(b, n)
                    if n == GT_AT:
                        make_gT(b)
                    deferred(n)
                    if former is not None and n == ACCT_AT:
                        make_accT(former)
                    if n == XT_AT:
                        make_xT(b + 1, (z_step, 1) if former is None else None)
                    if n == QK_AT:
                        make_qk(b + 1, (v_ready, 1) if former is None else (ln2_step, former * LN2 + LN2))
                    if n == UP0_AT:
                        if former is None:
                            pe.wait_ge(stage_used, 4)
                        up(b, 0)

            setup()
            make_xT(0)
            make_qk(0)
            make_v_logits(0)
            for n in range(UNITS):
                max_scores(0, n)
            make_mT(0)
            softmax_phase(0)

            with pe.Fori(0, NB - 1) as i:
                for n in range(NCH):
                    if n > 0:
                        up(i, n)
                    if n == 1:
                        make_v_logits(i + 1)
                    if has_max_unit(n):
                        max_scores(i + 1, n - MAX0)
                    if n >= LAG:
                        down(i, n - LAG, (v_ready, i + 2))
                    if n == WO_AT:
                        attn_out(i, (z_step, i * ZST + ZST + 1))
                    if n == MT_AT:
                        make_mT(i + 1)
                softmax_phase(i + 1, i)

            for n in range(NCH):
                if n > 0:
                    up(NB - 1, n)
                if n == WO_AT:
                    attn_out(NB - 1, (qk_split, NB * 4 + 4))
                if n >= LAG:
                    down(NB - 1, n - LAG, (qk_split, NB * 4 + 2))
            for n in range(NCH - LAG, NCH):
                down(NB - 1, n)
            make_accT(NB - 1)


def kernel(**inputs):
    import concourse.bacc as _bacc
    from concourse import mybir as _mybir
    from concourse.bass_utils import run_bass_kernel_spmd as _run

    a = {n: np.ascontiguousarray(v) for n, v in inputs.items()}
    chan = np.arange(D).reshape(4, PL, HD).transpose(2, 1, 0).reshape(-1)
    laid = {
        "x": a["L0_attn_x"],
        "wq": a["L0_attn_Wq"][:, chan], "bq": a["L0_attn_bq"][chan].reshape(D, 1),
        "wk": a["L0_attn_Wk"], "bk": a["L0_attn_bk"].reshape(D, 1),
        "wv": a["L0_attn_Wv"], "bv": a["L0_attn_bv"].reshape(D, 1),
        "wl": a["L0_attn_Wl"], "wlp": a["L0_attn_Wl"][:, chan],
        "bl": a["L0_attn_bl"], "blp": a["L0_attn_bl"][chan].reshape(D, 1),
        "wo": a["L0_attn_Wo"][chan, :], "bo": a["L0_attn_bo"],
        "gate_w": a["L0_ffn_gate_w"], "gate_b": a["L0_ffn_gate_b"],
        "w1": a["L0_ffn_w1"], "b1t": a["L0_ffn_b1"].reshape(NCH, P).T,
        "w2": a["L0_ffn_w2"], "b2t": a["L0_ffn_b2"].T,
        "ln_g": a["L0_ffn_ln_g"], "ln_b": a["L0_ffn_ln_b"],
    }
    nc = _bacc.Bacc("TRN2", target_bir_lowering=False, num_devices=1)
    arrays, args = {}, []
    for name, v in laid.items():
        v = np.ascontiguousarray(v)
        arrays["in_" + name] = v
        args.append(nc.dram_tensor("in_" + name, v.shape, _mybir.dt.from_np(v.dtype), kind="ExternalInput").ap())
    out = nc.dram_tensor("out", a["L0_attn_x"].shape, _mybir.dt.float32, kind="ExternalOutput").ap()
    build(nc, *args, out)
    r = _run(nc, [arrays], core_ids=[0])
    return r.results[0]["out"]
```

```python
from contextlib import ExitStack

import numpy as np

import concourse.bass as bass
from concourse import mybir
from concourse.alu_op_type import AluOpType as ALU

F32 = mybir.dt.float32
F32R = mybir.dt.float32r
ACT = mybir.ActivationFunctionType
AX = mybir.AxisListType

P = 128
D = 128
SEQ = 256
BLK = 512
T = BLK // P
H = 16
HD = D // H
PL = H // 4
E = 8
FF = 512
FC = FF // P
NCH = E * FC
EPS = 1e-5
TEMP = 0.9
SCALE = 1.0 / float(np.sqrt(HD))

RING = 10
HRING = 4
LAG = 8
GATE_LAG = 2
DVE_CHUNKS = (0, 2, 4, 6)
PSLOTS = 2
UNITS = H
MAX0 = 10
GT_AT = 2
NORM_AT = 6
WO_AT = 10
STORE_AT = 18
MT_AT = 28
STAGE = 6
DOWN_AT = (-1, -1, -1, 0, 1, 2, 3, 4)
ACCT_AT = 6
XT_AT = 7
Q_AT = 11
K_AT = 11
GEXP_AT = 14
UP0_AT = 13


def build(nc, x, wq, bq, wk, bk, wv, bv, wl, wlp, bl, blp, wo, bo, gate_w, gate_b, w1, b1t, w2, b2t,
          ln_g, ln_b, out):
    NB = x.shape[0] * x.shape[1] // BLK
    x_blk = x.rearrange("(b s) (p u) d -> b p s (u d)", s=2, u=2)
    out_blk = out.rearrange("(b s) (p u) d -> b p s (u d)", s=2, u=2)

    with ExitStack() as ctx:
        def sb(name, shape, dt=F32):
            return ctx.enter_context(nc.sbuf_tensor(name, shape, dt))

        def ps(name, shape):
            return ctx.enter_context(nc.psum_tensor(name, shape, F32))

        def sem(name):
            return ctx.enter_context(nc.semaphore(name))

        q_dram = nc.dram_tensor("q_dram", [4, 32, PL, BLK], F32).ap()
        k_dram = nc.dram_tensor("k_dram", [4, 32, PL, BLK], F32).ap()
        m_dram = nc.dram_tensor("m_dram", [4, PL, BLK], F32).ap()
        g_dram = nc.dram_tensor("g_dram", [E, BLK], F32).ap()
        o_dram = nc.dram_tensor("o_dram", [4, 32, PL, BLK], F32).ap()

        w1_hi, w1_lo = sb("w1_hi", [P, NCH, P], F32R), sb("w1_lo", [P, NCH, P], F32R)
        w2_hi, w2_lo = sb("w2_hi", [P, NCH, P], F32R), sb("w2_lo", [P, NCH, P], F32R)
        wq_hi, wq_lo = sb("wq_hi", [P, D], F32R), sb("wq_lo", [P, D], F32R)
        wk_hi, wk_lo = sb("wk_hi", [P, D], F32R), sb("wk_lo", [P, D], F32R)
        wv_hi, wv_lo = sb("wv_hi", [P, D], F32R), sb("wv_lo", [P, D], F32R)
        gw_hi, gw_lo = sb("gw_hi", [P, E], F32R), sb("gw_lo", [P, E], F32R)
        wo_sb = sb("wo_sb", [P, D])
        cols = sb("cols", [P, 4])
        bv_col = sb("bv_col", [P, 1])
        b1_sb = sb("b1_sb", [P, NCH])
        b2_sb = sb("b2_sb", [P, E])
        gb_bc = sb("gb_bc", [P, E])
        v_bias = sb("v_bias", [P, D])
        res_bias = sb("res_bias", [P, D])
        lng_bc = sb("lng_bc", [P, D])
        ident = sb("ident", [P, P])
        gw_raw = sb("gw_raw", [P, E])
        before = sb("before", [P, E, E])
        pause = sb("pause", [P, 1])
        half = sb("half", [P, T])

        x_sb = sb("x_sb", [P, T, D])
        stats, mv, vare, rstd = sb("stats", [P, T, 6]), sb("mv", [P, T, 2]), sb("vare", [P, T]), sb("rstd", [P, T])
        xn = sb("xn", [P, T, D])
        xT = sb("xT", [P, 2, BLK], F32R)
        Qs, Ks = sb("Qs", [P, PL, BLK], F32R), sb("Ks", [P, PL, BLK], F32R)
        V1 = sb("V1", [P, T, H, 2 * HD])
        mx = sb("mx", [P, T, H])
        mT = sb("mT", [H, BLK], F32R)
        prob = sb("prob", [P, PSLOTS, 2, BLK])
        o_sb = sb("o_sb", [P, PL, BLK])
        num, den = sb("num", [P, BLK]), sb("den", [P, BLK])
        xres, base = sb("xres", [P, T, D]), sb("base", [P, T, D])
        z0 = sb("z0", [P, T, E])
        z, gexp, gate = sb("z", [P, T, E]), sb("gexp", [P, T, E]), sb("gate", [P, T, E])
        keep, gmax, gsum = sb("keep", [P, T, E]), sb("gmax", [P, T]), sb("gsum", [P, T])
        cmp_a, cmp_b = sb("cmp_a", [P, T, E, E]), sb("cmp_b", [P, T, E, E])
        gT = sb("gT", [E, BLK])
        G = sb("G", [P, E, BLK])
        h = sb("h", [P, HRING, BLK])
        h_hi, h_lo = sb("h_hi", [P, RING, BLK], F32R), sb("h_lo", [P, RING, BLK], F32R)
        q_hl, k_hl = h_hi[:, STAGE:STAGE + 2, :], h_hi[:, STAGE + 2:STAGE + 4, :]
        y_g, accT = sb("y_g", [P, BLK]), sb("accT", [P, BLK])
        stats2, mv2, vare2, rstd2 = sb("stats2", [P, T, 6]), sb("mv2", [P, T, 2]), sb("vare2", [P, T]), sb("rstd2", [P, T])
        fin = sb("fin", [P, T, D])

        up_ps = ps("up_ps", [P, 2, BLK])
        y_ps = ps("y_ps", [P, 2, BLK])
        s_ps = ps("s_ps", [P, 2, 2, BLK])
        a_ps, b_ps = y_ps[:, 0, :], y_ps[:, 1, :]
        mT_ps = s_ps[0:H, 0, 0, :]

        w_in = sem("w_in")
        stage_in = [sem("stage_in0"), sem("stage_in1")]
        w_ready = [sem(f"w_ready{n}") for n in range(4)]
        small_ready = sem("small_ready")
        const_ready = sem("const_ready")
        dve_const = sem("dve_const")
        setup_pe = sem("setup_pe")
        x_in = sem("x_in")
        ln1_step = sem("ln1_step")
        rstd_ready = sem("rstd_ready")
        xn_ready = sem("xn_ready")
        xres_ready = sem("xres_ready")
        xT_ps_ready = sem("xT_ps_ready")
        xT_step = sem("xT_step")
        qkvg_ps = sem("qkvg_ps")
        strips_set = sem("strips_set")
        strips_stored = sem("strips_stored")
        qk_split = sem("qk_split")
        v_ready = sem("v_ready")
        z_step = sem("z_step")
        keep_step = sem("keep_step")
        qk_stored = sem("qk_stored")
        qk_loaded = [sem("qk_loaded0"), sem("qk_loaded1")]
        scores_ready = sem("scores_ready")
        max_done = sem("max_done")
        mT_ps_ready = sem("mT_ps_ready")
        mT_ready = sem("mT_ready")
        m_stored = sem("m_stored")
        m_loaded = sem("m_loaded")
        exp_done = sem("exp_done")
        av_done = sem("av_done")
        o_out = sem("o_out")
        o_stored = sem("o_stored")
        o_loaded = sem("o_loaded")
        norm_step = sem("norm_step")
        wo_ps_ready = sem("wo_ps_ready")
        base_ready = sem("base_ready")
        gexp_ready = sem("gexp_ready")
        gate_step = sem("gate_step")
        gT_ps_ready = sem("gT_ps_ready")
        gT_ready = sem("gT_ready")
        g_stored = sem("g_stored")
        g_loaded = sem("g_loaded")
        up_done = sem("up_done")
        gelu_done = sem("gelu_done")
        lo_done = sem("lo_done")
        split_step = sem("split_step")
        down_done = sem("down_done")
        acc_step = sem("acc_step")
        accT_ps_ready = sem("accT_ps_ready")
        ln2_step = sem("ln2_step")
        rstd2_ready = sem("rstd2_ready")
        fin_step = sem("fin_step")
        out_done = sem("out_done")

        W_SMALL = 16 * 18
        LN1, LN2, ZST, KEEP, GST, NORM = 3, 4, 3, 6, 4, 2
        ACC = 2 * E

        def unit(n):
            return n // 4, n % 2 * 2, n // 2 % 2

        def gelus(b, n):
            return b * (2 * NCH - len(DVE_CHUNKS)) + 2 * (n + 1) - sum(m <= n for m in DVE_CHUNKS)

        def lows(b, n):
            return b * (NCH - len(DVE_CHUNKS)) + n + 1 - sum(m <= n for m in DVE_CHUNKS)

        def split_of(b, n):
            if n in DVE_CHUNKS:
                return split_step, b * 2 * len(DVE_CHUNKS) + 2 * DVE_CHUNKS.index(n) + 2
            return lo_done, lows(b, n)

        def split_w(engine, n):
            stage = G[:, 4 * (n % 2):4 * (n % 2) + 4, :].rearrange("p a (b c) -> p (a b) c", c=P)
            hi, lo = ((w1_hi, w1_lo), (w2_hi, w2_lo))[n // 2]
            at = slice(16 * (n % 2), 16 * (n % 2) + 16)
            engine.wait_ge(stage_in[n % 2], 16 * (n // 2) + 16)
            engine.tensor_copy(hi[:, at, :], stage).then_inc(w_ready[n], 1)
            engine.wait_ge(w_ready[n], 1)
            engine.tensor_tensor(lo[:, at, :], stage, hi[:, at, :].bitcast(F32), ALU.subtract).then_inc(w_ready[n], 1)

        def has_max_unit(n):
            return MAX0 <= n < MAX0 + UNITS

        w1_v = w1.rearrange("e d f -> d e f")
        w2_v = w2.rearrange("e (c p) d -> p (e c) d", p=P)
        halves = [w1_v[:, 0:4, :], w1_v[:, 4:8, :], w2_v[:, 0:16, :], w2_v[:, 16:32, :]]

        block = ctx.enter_context(nc.Block())

        @block.sync
        def _(sp):
            sp.dma_start(x_sb[:, :, :].rearrange("p (s u) d -> p s (u d)", s=2), x_blk[0]).then_inc(x_in, 16)
            for dst, src in ((cols[:, 0:1], bq), (cols[:, 1:2], bk), (cols[:, 2:3], blp), (bv_col[:, :], bv),
                             (xn[:, 0, :], wq), (xn[:, 1, :], wk), (xn[:, 2, :], wv), (xn[:, 3, :], wl),
                             (xres[:, 0, :], wlp)):
                sp.dma_start(dst, src).then_inc(w_in, 16)
            for n in range(2):
                sp.dma_start(G[:, 4 * n:4 * n + 4, :], halves[n]).then_inc(stage_in[n], 16)

            def store_qk():
                for dram, t, src in ((q_dram, q_hl, (0, 0, 1)), (k_dram, k_hl, (0, 1, 0))):
                    for c in range(3):
                        sp.dma_start(dram[:, 8 * c:8 * c + 8, :, :].rearrange("j r g n -> (r g) j n"),
                                     t[:, src[c], :].bitcast(F32)).then_inc(qk_stored, 16)

            def load_qk(side):
                planes = slice(side * PL // 2, (side + 1) * PL // 2)
                for strips, dram in ((Qs, q_dram), (Ks, k_dram)):
                    sp.dma_start(strips[:, planes, :].bitcast(F32),
                                 dram[:, :, planes, :].rearrange("j r g n -> (j r) g n")).then_inc(qk_loaded[side], 16)

            def load_g():
                sp.dma_start(G[:, :, :], g_dram.partition_broadcast(P)).then_inc(g_loaded, 16)

            def store_o(planes):
                sp.dma_start(o_dram[:, :, planes, :].rearrange("j r g n -> (j r) g n"), o_sb[:, planes, :]).then_inc(o_stored, 16)

            def block_moves(b, x_next, last=False):
                s = (lambda v: v) if isinstance(b, int) else sp.snap
                w_1, w_16, w_split, w_qks = s(b + 1), s(b * 16 + 16), s(b * 4 + 8), s(b * 96 + 192)
                w_ohalf, w_olast, w_o2 = s(b * 4 + 2), s(b * 4 + 4), s(b * 32 + 32)
                w_acc, w_scores = s(b * ACC + ACC), s(b * 2 * UNITS + 2 * UNITS)
                w_gT, w_g = s(b + 2), s(b * 16 + 32)
                sp.wait_ge(xres_ready, w_1)
                sp.dma_start(x_sb[:, :, :].rearrange("p (s u) d -> p s (u d)", s=2), x_next).then_inc(x_in, 16)
                sp.wait_ge(mT_ready, w_1)
                sp.dma_start(m_dram.rearrange("j g n -> (j g) n"), mT[:, :].bitcast(F32)).then_inc(m_stored, 16)
                sp.wait_ge(m_stored, w_16)
                sp.dma_start(Qs[24:P:32, :, :].bitcast(F32), m_dram).then_inc(m_loaded, 16)
                sp.wait_ge(o_out, w_ohalf)
                store_o(slice(0, PL // 2))
                if not last:
                    sp.wait_ge(qk_split, w_split)
                    store_qk()
                sp.wait_ge(o_out, w_olast)
                store_o(slice(PL // 2, PL))
                sp.wait_ge(o_stored, w_o2)
                sp.dma_start(num[:, :], o_dram[:, 0:8, :, :].rearrange("j r g n -> (r g) j n")).then_inc(o_loaded, 16)
                sp.dma_start(den[:, :], o_dram[:, 8:16, :, :].rearrange("j r g n -> (r g) j n")).then_inc(o_loaded, 16)
                if not last:
                    sp.wait_ge(qk_stored, w_qks)
                    sp.wait_ge(scores_ready, w_scores)
                    load_qk(0)
                    sp.wait_ge(gT_ready, w_gT)
                    sp.dma_start(g_dram, gT[:, :]).then_inc(g_stored, 16)
                    sp.wait_ge(g_stored, w_g)
                    sp.wait_ge(acc_step, w_acc)
                    load_g()
                    load_qk(1)

            sp.wait_ge(qk_split, 4)
            store_qk()
            sp.wait_ge(gT_ready, 1)
            sp.dma_start(g_dram, gT[:, :]).then_inc(g_stored, 16)
            sp.wait_ge(qk_stored, 96)
            sp.wait_ge(strips_stored, 128)
            load_qk(0)
            load_qk(1)
            sp.wait_ge(g_stored, 16)
            for n in range(4):
                sp.wait_ge(w_ready[n], 2)
            load_g()
            block_moves(0, x_blk[1])
            with sp.Fori(0, NB - 2) as i:
                block_moves(i + 1, x_blk[2:NB][i])
            block_moves(NB - 1, x_blk[NB - 1], last=True)

        @block.gpsimd
        def _(pool):
            nc.gpsimd.memset(ident[:, :], 0.0)
            nc.gpsimd.memset(before[:, :, :], 1.0)
            nc.gpsimd.memset(half[:, :], -0.5).then_inc(const_ready, 1)
            pool.wait_ge(const_ready, 1)
            nc.gpsimd.affine_select(out=ident[:, :], in_=ident[:, :], compare_op=ALU.not_equal, fill=1.0,
                                    base=0, pattern=[[-1, P]], channel_multiplier=1).then_inc(const_ready, 1)
            nc.gpsimd.affine_select(out=before[:, :, :], in_=before[:, :, :], compare_op=ALU.is_gt, fill=0.0,
                                    base=0, pattern=[[1, E], [-1, E]], channel_multiplier=0).then_inc(const_ready, 1)
            pool.wait_ge(const_ready, 3)

            def rstd_of(b):
                pool.wait_ge(ln1_step, b * LN1 + 3)
                nc.gpsimd.tensor_tensor(rstd[:, :], vare[:, :], half[:, :], ALU.pow).then_inc(rstd_ready, 1)

            def residual(b, first):
                if not first:
                    pool.wait_ge(base_ready, b)
                pool.wait_ge(x_in, b * 16 + 16)
                nc.gpsimd.tensor_tensor(xres[:, :, :], x_sb[:, :, :], res_bias[:, :].unsqueeze(1).broadcast_to((P, T, D)),
                                        ALU.add).then_inc(xres_ready, 1)

            def low_part(b, n):
                pool.wait_ge(gelu_done, gelus(b, n))
                if n >= RING:
                    pool.wait_ge(down_done, b * NCH + n - RING + 1)
                nc.gpsimd.tensor_tensor(h_lo[:, n % RING, :], h[:, n % HRING, :], h_hi[:, n % RING, :].bitcast(F32),
                                        ALU.subtract).then_inc(lo_done, 1)

            def rstd2_of(b):
                pool.wait_ge(ln2_step, b * LN2 + 3)
                nc.gpsimd.tensor_tensor(rstd2[:, :], vare2[:, :], half[:, :], ALU.pow).then_inc(rstd2_ready, 1)

            def scale(b):
                pool.wait_ge(ln2_step, b * LN2 + 4)
                nc.gpsimd.tensor_tensor(fin[:, :, :], fin[:, :, :], lng_bc[:, :].unsqueeze(1).broadcast_to((P, T, D)),
                                        ALU.mult).then_inc(fin_step, 1)

            def add_base(b):
                pool.wait_ge(base_ready, b + 1)
                pool.wait_ge(fin_step, b * 2 + 1)
                nc.gpsimd.tensor_tensor(fin[:, :, :], fin[:, :, :], base[:, :, :], ALU.add).then_inc(fin_step, 1)

            def turn(b, first):
                for n in range(NCH):
                    if n not in DVE_CHUNKS:
                        low_part(b, n)
                    if n == WO_AT + 1:
                        if not first:
                            add_base(b - 1)
                        residual(b, first)
                rstd_of(b + 1)
                rstd2_of(b)
                scale(b)

            rstd_of(0)
            split_w(nc.gpsimd, 1)
            pool.wait_ge(small_ready, 1)
            turn(0, True)
            with pool.Fori(1, NB) as i:
                turn(i, False)
            add_base(NB - 1)

        @block.scalar
        def _(act):
            for dst, src in ((wo_sb[:, :], wo), (gw_raw[:, :], gate_w), (b1_sb[:, :], b1t),
                             (b2_sb[:, :], b2t), (gb_bc[:, :], gate_b.partition_broadcast(P)),
                             (xres[:, 1, :], bl.partition_broadcast(P)), (res_bias[:, :], bo.partition_broadcast(P)),
                             (xres[:, 2, :], ln_b.partition_broadcast(P)), (lng_bc[:, :], ln_g.partition_broadcast(P))):
                act.dma_start(dst, src).then_inc(w_in, 16)
            act.wait_ge(strips_set, 1)
            for dram in (q_dram, k_dram):
                for j in range(4):
                    act.dma_start(dram[j, 24:32], Ks[0:8, :, :].bitcast(F32)).then_inc(strips_stored, 16)
            act.wait_ge(small_ready, 1)

            def gate_exp(b):
                act.wait_ge(z_step, b * ZST + 2)
                nc.scalar.activation(gexp[:, :, :], z0[:, :, :], ACT.Exp, scale=1.0 / TEMP).then_inc(gexp_ready, 1)

            def softmax_exp(b, n):
                act.wait_ge(scores_ready, b * 2 * UNITS + UNITS + n + 1)
                if n >= PSLOTS:
                    act.wait_ge(av_done, b * UNITS + n - PSLOTS + 1)
                nc.scalar.activation(prob[:, n % PSLOTS], s_ps[:, n % 2], ACT.Exp, scale=SCALE).then_inc(exp_done, 1)

            def gelu(b, n, stage_free):
                act.wait_ge(up_done, b * NCH + n + 1)
                if n >= HRING:
                    act.wait_ge(*split_of(b, n - HRING))
                nc.scalar.activation(h[:, n % HRING, :], up_ps[:, n % 2, :], ACT.Gelu, bias=b1_sb[:, n:n + 1]).then_inc(gelu_done, 1)
                if n in DVE_CHUNKS:
                    return
                if n == STAGE + 1:
                    act.wait_ge(*stage_free)
                if n >= RING:
                    act.wait_ge(down_done, b * NCH + n - RING + 1)
                nc.scalar.activation(h_hi[:, n % RING, :], up_ps[:, n % 2, :], ACT.Gelu, bias=b1_sb[:, n:n + 1]).then_inc(gelu_done, 1)

            def store_out(b):
                act.wait_ge(fin_step, b * 2 + 2)
                act.dma_start(out_blk[b], fin[:, :, :].rearrange("p (s u) d -> p s (u d)", s=2)).then_inc(out_done, 16)

            def turn(b, first):
                for n in range(NCH):
                    gelu(b, n, (qk_stored, b * 96 + 96))
                    if n == STORE_AT and not first:
                        store_out(b - 1)
                for n in range(UNITS):
                    softmax_exp(b, n)
                    if n == GEXP_AT:
                        gate_exp(b + 1)

            for n in range(2):
                act.wait_ge(w_ready[n], 2)
                act.dma_start(G[:, 4 * n:4 * n + 4, :].rearrange("p a (b c) -> p (a b) c", c=P),
                              halves[2 + n]).then_inc(stage_in[n], 16)
            gate_exp(0)
            turn(0, True)
            with act.Fori(1, NB) as i:
                turn(i, False)
            store_out(NB - 1)
            act.wait_ge(out_done, 16 * NB)

        @block.vector
        def _(dve):
            def setup():
                count = [0]

                def step(ins):
                    count[0] += 1
                    ins.then_inc(dve_const, 1)

                def stepped():
                    dve.wait_ge(dve_const, count[0])

                nc.vector.memset(Ks[:, :, :].bitcast(F32), -1.0).then_inc(strips_set, 1)
                nc.vector.memset(up_ps[:, :, :], 0.0)
                step(nc.vector.memset(V1[:, :, :, HD:2 * HD], 1.0))
                dve.wait_ge(w_in, W_SMALL)
                step(nc.vector.tensor_copy(base[:, 0, :], bv_col[:, :].broadcast_to((P, D))))
                assert count[0] == 2
                nc.vector.tensor_copy(wq_hi[:, :], xn[:, 0, :])
                step(nc.vector.tensor_copy(gw_hi[:, :], gw_raw[:, :]))
                stepped()
                nc.vector.tensor_tensor(wq_lo[:, :], xn[:, 0, :], wq_hi[:, :].bitcast(F32), ALU.subtract)
                nc.vector.tensor_tensor(gw_lo[:, :], gw_raw[:, :], gw_hi[:, :].bitcast(F32), ALU.subtract)
                nc.vector.tensor_tensor(res_bias[:, :], res_bias[:, :], xres[:, 2, :], ALU.add)
                dve.wait_ge(setup_pe, 1)
                nc.vector.tensor_copy(base[:, 1:3, :], a_ps[:, 0:2 * D].rearrange("p (a b) -> p a b", a=2)).then_inc(dve_const, 1)
                count[0] += 1
                assert count[0] == 4
                dve.wait_ge(setup_pe, 2)
                nc.vector.tensor_copy(wk_hi[:, :], b_ps[:, 0:D])
                step(nc.vector.tensor_copy(wv_hi[:, :], b_ps[:, D:2 * D]))
                stepped()
                nc.vector.tensor_tensor(wk_lo[:, :], b_ps[:, 0:D], wk_hi[:, :].bitcast(F32), ALU.subtract)
                nc.vector.tensor_tensor(wv_lo[:, :], b_ps[:, D:2 * D], wv_hi[:, :].bitcast(F32), ALU.subtract)
                nc.vector.tensor_tensor(v_bias[:, :], b_ps[:, 2 * D:3 * D], xres[:, 1, :], ALU.add)
                nc.vector.tensor_tensor(cols[:, 3:4], b_ps[:, 3 * D:3 * D + 1], cols[:, 2:3], ALU.add).then_inc(small_ready, 1)
                dve.wait_ge(small_ready, 1)

            def norm_stats(b, src, st, agg, ve, steps, per):
                for t in range(T):
                    last = nc.vector.bn_stats(st[:, t, :], src(t))
                last.then_inc(steps, 1)
                dve.wait_ge(steps, b * per + 1)
                nc.vector.memset(pause[:, :], 0.0)
                for t in range(T):
                    last = nc.vector.bn_aggr(agg[:, t, :], st[:, t, :])
                last.then_inc(steps, 1)
                dve.wait_ge(steps, b * per + 2)
                nc.vector.tensor_scalar(ve[:, :], agg[:, :, 1], EPS, None, ALU.add).then_inc(steps, 1)

            def ln1_stats(b):
                dve.wait_ge(x_in, b * 16 + 16)
                norm_stats(b, lambda t: x_sb[:, t, :], stats, mv, vare, ln1_step, LN1)

            def ln1_apply(b):
                dve.wait_ge(rstd_ready, b + 1)
                for t in range(T):
                    last = nc.vector.tensor_scalar(xn[:, t, :], x_sb[:, t, :], mv[:, t, 0:1], rstd[:, t:t + 1],
                                                   ALU.subtract, ALU.mult)
                last.then_inc(xn_ready, 1)

            def take_xT(b):
                dve.wait_ge(xT_ps_ready, b + 1)
                nc.vector.tensor_copy(xT[:, 0, :], b_ps).then_inc(xT_step, 1)
                dve.wait_ge(xT_step, b * 2 + 1)
                nc.vector.tensor_tensor(xT[:, 1, :], b_ps, xT[:, 0, :].bitcast(F32), ALU.subtract).then_inc(xT_step, 1)

            def split_qk(b):
                for m, (ps_, bias, hl) in enumerate(((a_ps, cols[:, 0:1], q_hl), (b_ps, cols[:, 3:4], k_hl))):
                    dve.wait_ge(qkvg_ps, b * 4 + 2 * m + 1)
                    nc.vector.tensor_scalar(hl[:, 0, :], ps_, bias, None, ALU.add).then_inc(qk_split, 1)
                    dve.wait_ge(qk_split, b * 4 + 2 * m + 1)
                    nc.vector.scalar_tensor_tensor(hl[:, 1, :], ps_, bias, hl[:, 0, :].bitcast(F32), ALU.add,
                                                   ALU.subtract).then_inc(qk_split, 1)

            def take_v(b):
                dve.wait_ge(qkvg_ps, b * 4 + 4)
                nc.vector.tensor_tensor(V1[:, :, :, 0:HD], a_ps.rearrange("p (t h d) -> p t h d", t=T, h=H),
                                        v_bias[:, :].rearrange("p (h d) -> p h d", h=H).unsqueeze(1).broadcast_to((P, T, H, HD)),
                                        ALU.add).then_inc(v_ready, 1)

            def take_logits(b):
                dve.wait_ge(qkvg_ps, b * 4 + 2)
                nc.vector.tensor_tensor(z[:, :, :], b_ps[:, 0:T * E].rearrange("p (t e) -> p t e", t=T),
                                        gb_bc[:, :].unsqueeze(1).broadcast_to((P, T, E)), ALU.add).then_inc(z_step, 1)
                dve.wait_ge(z_step, b * ZST + 1)
                nc.vector.tensor_reduce(gmax[:, :], z[:, :, :], axis=AX.X, op=ALU.max).then_inc(keep_step, 1)
                dve.wait_ge(keep_step, b * KEEP + 1)
                nc.vector.tensor_tensor(z0[:, :, :], z[:, :, :], gmax[:, :].unsqueeze(2).broadcast_to((P, T, E)),
                                        ALU.subtract).then_inc(z_step, 1)

            def rank(b):
                mine = z[:, :, :].unsqueeze(3).broadcast_to((P, T, E, E))
                other = z[:, :, :].unsqueeze(2).broadcast_to((P, T, E, E))
                nc.vector.tensor_tensor(cmp_a[:, :, :, :], other, mine, ALU.is_equal).then_inc(keep_step, 1)
                nc.vector.tensor_tensor(cmp_b[:, :, :, :], other, mine, ALU.is_gt).then_inc(keep_step, 1)
                dve.wait_ge(keep_step, b * KEEP + 2)
                nc.vector.tensor_tensor(cmp_a[:, :, :, :].rearrange("p t e f -> p t (e f)"),
                                        cmp_a[:, :, :, :].rearrange("p t e f -> p t (e f)"),
                                        before[:, :, :].rearrange("p e f -> p (e f)").unsqueeze(1).broadcast_to((P, T, E * E)),
                                        ALU.mult).then_inc(keep_step, 1)
                dve.wait_ge(keep_step, b * KEEP + 4)
                nc.vector.tensor_tensor(cmp_a[:, :, :, :], cmp_a[:, :, :, :], cmp_b[:, :, :, :], ALU.add).then_inc(keep_step, 1)
                dve.wait_ge(keep_step, b * KEEP + 5)
                nc.vector.tensor_reduce(keep[:, :, :], cmp_a[:, :, :, :], axis=AX.X, op=ALU.add).then_inc(keep_step, 1)
                dve.wait_ge(keep_step, b * KEEP + 6)
                nc.vector.tensor_scalar(keep[:, :, :], keep[:, :, :], 1.5, None, ALU.is_lt).then_inc(z_step, 1)

            def take_max(b, n):
                g, j, s = unit(n)
                dve.wait_ge(scores_ready, b * 2 * UNITS + n + 1)
                heads = slice(4 * j + g, 4 * j + g + 5, 4)
                nc.vector.tensor_reduce(mx[:, 2 * s:2 * s + 2, heads].rearrange("p u j -> p j u"),
                                        s_ps[:, n % 2].rearrange("p j (u k) -> p j u k", u=2),
                                        axis=AX.X, op=ALU.max).then_inc(max_done, 1)

            def take_mT(b, first):
                dve.wait_ge(mT_ps_ready, b + 1)
                if not first:
                    dve.wait_ge(m_stored, b * 16)
                nc.vector.tensor_copy(mT[:, :], mT_ps).then_inc(mT_ready, 1)

            def gates(b):
                dve.wait_ge(gexp_ready, b + 1)
                dve.wait_ge(z_step, b * ZST + 3)
                nc.vector.tensor_tensor(gexp[:, :, :], gexp[:, :, :], keep[:, :, :], ALU.mult).then_inc(gate_step, 1)
                dve.wait_ge(gate_step, b * GST + 1)
                nc.vector.tensor_reduce(gsum[:, :], gexp[:, :, :], axis=AX.X, op=ALU.add).then_inc(gate_step, 1)
                dve.wait_ge(gate_step, b * GST + 2)
                nc.vector.reciprocal(gsum[:, :], gsum[:, :]).then_inc(gate_step, 1)
                dve.wait_ge(gate_step, b * GST + 3)
                nc.vector.tensor_tensor(gate[:, :, :], gexp[:, :, :], gsum[:, :].unsqueeze(2).broadcast_to((P, T, E)),
                                        ALU.mult).then_inc(gate_step, 1)

            def take_gT(b, first):
                dve.wait_ge(gT_ps_ready, b + 1)
                if not first:
                    dve.wait_ge(g_stored, b * 16)
                nc.vector.tensor_copy(gT[:, :], b_ps[0:E, :]).then_inc(gT_ready, 1)

            def take_o(b, g, first):
                dve.wait_ge(av_done, b * UNITS + 4 * g + 4)
                if g == 0 and not first:
                    dve.wait_ge(o_stored, b * 32)
                nc.vector.tensor_copy(o_sb[:, g, :], up_ps[:, g % 2, :]).then_inc(o_out, 1)

            def attn_norm(b):
                dve.wait_ge(o_loaded, b * 32 + 32)
                nc.vector.reciprocal(den[:, :], den[:, :]).then_inc(norm_step, 1)
                dve.wait_ge(norm_step, b * NORM + 1)
                nc.vector.tensor_tensor(num[:, :], num[:, :], den[:, :], ALU.mult).then_inc(norm_step, 1)

            def attn_add(b, base_used):
                dve.wait_ge(wo_ps_ready, b + 1)
                dve.wait_ge(xres_ready, b + 1)
                dve.wait_ge(*base_used)
                nc.vector.tensor_tensor(base[:, :, :], b_ps.rearrange("p (t d) -> p t d", t=T), xres[:, :, :],
                                        ALU.add).then_inc(base_ready, 1)

            def split_h(b, n, stage_free):
                if n == STAGE:
                    dve.wait_ge(*stage_free)
                dve.wait_ge(gelu_done, gelus(b, n))
                nc.vector.tensor_copy(h_hi[:, n % RING, :], h[:, n % HRING, :]).then_inc(split_step, 1)
                dve.wait_ge(split_step, split_of(b, n)[1] - 1)
                nc.vector.tensor_tensor(h_lo[:, n % RING, :], h[:, n % HRING, :], h_hi[:, n % RING, :].bitcast(F32),
                                        ALU.subtract).then_inc(split_step, 1)

            def gate_y(b, e):
                if e == 0:
                    dve.wait_ge(g_loaded, b * 16 + 16)
                dve.wait_ge(down_done, b * NCH + FC * (e + 1))
                if e >= 2:
                    dve.wait_ge(acc_step, b * ACC + 2 * e - 1)
                dst = accT[:, :] if e == 0 else y_g[:, :]
                nc.vector.scalar_tensor_tensor(dst, y_ps[:, e % 2, :], b2_sb[:, e:e + 1], G[:, e, :], ALU.add, ALU.mult).then_inc(acc_step, 1)

            def add_y(b, e):
                if e == 0:
                    return
                dve.wait_ge(acc_step, b * ACC + 2 * e)
                nc.vector.tensor_tensor(accT[:, :], accT[:, :], y_g[:, :], ALU.add).then_inc(acc_step, 2 if e == E - 1 else 1)

            def ln2_stats(b):
                dve.wait_ge(accT_ps_ready, b + 1)
                norm_stats(b, lambda t: a_ps[:, t * D:(t + 1) * D], stats2, mv2, vare2, ln2_step, LN2)

            def ln2_apply(b, first):
                dve.wait_ge(rstd2_ready, b + 1)
                if not first:
                    dve.wait_ge(out_done, b * 16)
                for t in range(T):
                    last = nc.vector.tensor_scalar(fin[:, t, :], a_ps[:, t * D:(t + 1) * D], mv2[:, t, 0:1],
                                                   rstd2[:, t:t + 1], ALU.subtract, ALU.mult)
                last.then_inc(ln2_step, 1)

            def turn(b, first):
                for n in range(NCH):
                    if n == 1:
                        take_v(b)
                    if n == GT_AT:
                        take_gT(b, first)
                    if first and n == NORM_AT:
                        split_w(nc.vector, 3)
                    if n in DVE_CHUNKS:
                        split_h(b, n, (qk_stored, b * 96 + 96))
                    if n == NORM_AT and not first:
                        attn_norm(b - 1)
                    if n == WO_AT and not first:
                        attn_add(b - 1, (lo_done, lows(b, 1)))
                    e, at = divmod(n - LAG - GATE_LAG - FC, FC)
                    if e >= 0 and at == 0:
                        gate_y(b, e)
                    if has_max_unit(n):
                        take_max(b, n - MAX0)
                    if e >= 0 and at == 0:
                        add_y(b, e)
                    if n == MT_AT:
                        take_mT(b, first)
                for e in (E - 3, E - 2):
                    gate_y(b, e)
                    add_y(b, e)
                ln1_stats(b + 1)
                take_o(b, 0, first)
                gate_y(b, E - 1)
                add_y(b, E - 1)
                ln1_apply(b + 1)
                ln2_stats(b)
                take_o(b, 1, first)
                ln2_apply(b, first)
                take_xT(b + 1)
                take_o(b, 2, first)
                take_logits(b + 1)
                split_qk(b + 1)
                take_o(b, 3, first)
                rank(b + 1)
                gates(b + 1)

            ln1_stats(0)
            setup()
            ln1_apply(0)
            take_xT(0)
            take_logits(0)
            split_qk(0)
            split_w(nc.vector, 0)
            rank(0)
            gates(0)
            split_w(nc.vector, 2)
            turn(0, True)
            with dve.Fori(1, NB) as i:
                turn(i, False)
            attn_norm(NB - 1)
            attn_add(NB - 1, (fin_step, 2 * NB - 1))

        @block.tensor
        def _(pe):
            def split_product(dst, w_hi, w_lo, m_hi, m_lo, first=True, last=True):
                nc.tensor.matmul(dst, w_hi, m_hi, start=first, stop=False)
                nc.tensor.matmul(dst, w_lo, m_hi, start=False, stop=False)
                return nc.tensor.matmul(dst, w_hi, m_lo, start=False, stop=last)

            def setup():
                pe.wait_ge(const_ready, 3)
                pe.wait_ge(w_in, W_SMALL)
                nc.tensor.transpose(a_ps[:, 0:D], xn[:, 1, :], ident[:, :])
                nc.tensor.transpose(a_ps[:, D:2 * D], xn[:, 2, :], ident[:, :]).then_inc(setup_pe, 1)
                pe.wait_ge(dve_const, 4)
                nc.tensor.matmul(b_ps[:, 0:D], base[:, 1, :], xres[:, 0, :], start=True, stop=True)
                nc.tensor.matmul(b_ps[:, D:2 * D], base[:, 2, :], xn[:, 3, :], start=True, stop=True)
                nc.tensor.matmul(b_ps[:, 2 * D:3 * D], base[:, 0, :], xn[:, 3, :], start=True, stop=True)
                nc.tensor.matmul(b_ps[:, 3 * D:3 * D + 1], xres[:, 0, :], cols[:, 1:2], start=True, stop=True).then_inc(setup_pe, 1)
                pe.wait_ge(small_ready, 1)

            def make_xT(b):
                pe.wait_ge(xn_ready, b + 1)
                for t in range(T):
                    last = nc.tensor.transpose(b_ps[:, t * P:(t + 1) * P], xn[:, t, :], ident[:, :])
                last.then_inc(xT_ps_ready, 1)

            def make_q_logits(b, a_ps_used=None):
                pe.wait_ge(xT_step, b * 2 + 2)
                if a_ps_used is not None:
                    pe.wait_ge(*a_ps_used)
                split_product(a_ps, wq_hi[:, :], wq_lo[:, :], xT[:, 0, :], xT[:, 1, :]).then_inc(qkvg_ps, 1)
                for t in range(T):
                    tok = slice(t * P, (t + 1) * P)
                    last = split_product(b_ps[:, t * E:(t + 1) * E], xT[:, 0, tok], xT[:, 1, tok], gw_hi[:, :], gw_lo[:, :])
                last.then_inc(qkvg_ps, 1)

            def make_k(b):
                pe.wait_ge(z_step, b * ZST + 1)
                split_product(b_ps, wk_hi[:, :], wk_lo[:, :], xT[:, 0, :], xT[:, 1, :]).then_inc(qkvg_ps, 1)

            def make_v(b):
                pe.wait_ge(qk_split, b * 4 + 2)
                for t in range(T):
                    tok = slice(t * P, (t + 1) * P)
                    last = split_product(a_ps[:, tok], xT[:, 0, tok], xT[:, 1, tok], wv_hi[:, :], wv_lo[:, :])
                last.then_inc(qkvg_ps, 1)

            def max_scores(b, n):
                g, j, s = unit(n)
                if n == 0:
                    pe.wait_ge(qk_loaded[0], b * 32 + 32)
                if n == UNITS // 2:
                    pe.wait_ge(qk_loaded[1], b * 32 + 32)
                if n >= 2:
                    pe.wait_ge(max_done, b * UNITS + n - 1)
                for u in range(2):
                    for d in range(2):
                        rows = slice(32 * (j + d), 32 * (j + d) + 24)
                        last = nc.tensor.matmul(s_ps[:, n % 2, d, u * SEQ:(u + 1) * SEQ],
                                                Qs[rows, g, s * SEQ + u * P:s * SEQ + (u + 1) * P],
                                                Ks[rows, g, s * SEQ:(s + 1) * SEQ], start=True, stop=True)
                last.then_inc(scores_ready, 1)

            def make_mT(b):
                pe.wait_ge(max_done, b * UNITS + UNITS)
                for t in range(T):
                    last = nc.tensor.transpose(mT_ps[:, t * P:(t + 1) * P], mx[:, t, :], ident[:, :])
                last.then_inc(mT_ps_ready, 1)

            def soft_scores(b, n):
                g, j, s = unit(n)
                if n == 0:
                    pe.wait_ge(m_loaded, b * 16 + 16)
                if n >= 2:
                    pe.wait_ge(exp_done, b * UNITS + n - 1)
                for u in range(2):
                    for d in range(2):
                        rows = slice(32 * (j + d), 32 * (j + d) + 25)
                        last = nc.tensor.matmul(s_ps[:, n % 2, d, u * SEQ:(u + 1) * SEQ],
                                                Ks[rows, g, s * SEQ + u * P:s * SEQ + (u + 1) * P],
                                                Qs[rows, g, s * SEQ:(s + 1) * SEQ], start=True, stop=True)
                last.then_inc(scores_ready, 1)

            def weigh(b, n):
                g, j, s = unit(n)
                if n % 4 == 0 and g >= 2:
                    pe.wait_ge(o_out, b * PL + g - 1)
                pe.wait_ge(exp_done, b * UNITS + n + 1)
                for u in range(2):
                    for d in range(2):
                        rows = slice(32 * (j + d), 32 * (j + d) + 2 * HD)
                        last = nc.tensor.matmul(up_ps[rows, g % 2, s * SEQ:(s + 1) * SEQ], V1[:, 2 * s + u, 4 * (j + d) + g, :],
                                                prob[:, n % PSLOTS, d, u * SEQ:(u + 1) * SEQ], start=u == 0, stop=u == 1)
                last.then_inc(av_done, 1)

            def make_gT(b):
                pe.wait_ge(gate_step, b * GST + 4)
                pe.wait_ge(qk_split, b * 4 + 4)
                for t in range(T):
                    last = nc.tensor.transpose(b_ps[0:E, t * P:(t + 1) * P], gate[:, t, :], ident[:, :])
                last.then_inc(gT_ps_ready, 1)

            def attn_out(b, b_ps_used):
                pe.wait_ge(norm_step, b * NORM + 2)
                pe.wait_ge(*b_ps_used)
                for t in range(T):
                    last = nc.tensor.matmul(b_ps[:, t * D:(t + 1) * D], num[:, t * P:(t + 1) * P], wo_sb[:, :],
                                            start=True, stop=True)
                last.then_inc(wo_ps_ready, 1)

            def up(b, n, bank_free=None):
                if bank_free is not None:
                    pe.wait_ge(*bank_free)
                elif n >= 2:
                    pe.wait_ge(gelu_done, gelus(b, n - 2))
                split_product(up_ps[:, n % 2, :], w1_hi[:, n, :], w1_lo[:, n, :], xT[:, 0, :], xT[:, 1, :]).then_inc(up_done, 1)

            def down(b, n, first):
                e, c = n // FC, n % FC
                pe.wait_ge(*split_of(b, n))
                if n == 0:
                    pe.wait_ge(v_ready, b + 1)
                if c == 0 and e == 1:
                    pe.wait_ge(*((gT_ready, 1) if first else (base_ready, b)))
                if c == 0 and e >= 2:
                    pe.wait_ge(acc_step, b * ACC + max(1, 2 * (e - 2)))
                split_product(y_ps[:, e % 2, :], w2_hi[:, n, :], w2_lo[:, n, :], h_hi[:, n % RING, :], h_lo[:, n % RING, :],
                              first=c == 0, last=c == FC - 1).then_inc(down_done, 1)

            def make_accT(b):
                pe.wait_ge(acc_step, b * ACC + ACC)
                for t in range(T):
                    last = nc.tensor.transpose(a_ps[:, t * D:(t + 1) * D], accT[:, t * P:(t + 1) * P], ident[:, :])
                last.then_inc(accT_ps_ready, 1)

            def turn(b, first):
                def deferred(n):
                    for m, at in enumerate(DOWN_AT):
                        if at == n:
                            down(b, NCH - LAG + m, first)

                for n in range(NCH):
                    if first and n == NCH // 2:
                        pe.wait_ge(w_ready[1], 2)
                    if n == 1:
                        up(b, n, None if first else (o_out, b * PL))
                        make_v(b)
                    if n > 1:
                        up(b, n)
                    if n == GT_AT:
                        make_gT(b)
                    if has_max_unit(n):
                        max_scores(b, n - MAX0)
                    if first and n in (LAG, LAG + NCH // 2):
                        pe.wait_ge(w_ready[2 + (n - LAG) // (NCH // 2)], 2)
                    if n >= LAG:
                        down(b, n - LAG, first)
                    if n == WO_AT and not first:
                        attn_out(b - 1, (gT_ready, b + 1))
                    if n == MT_AT:
                        make_mT(b)
                deferred(-1)
                soft_scores(b, 0)
                soft_scores(b, 1)
                for n in range(UNITS):
                    if n + 2 < UNITS:
                        soft_scores(b, n + 2)
                    weigh(b, n)
                    deferred(n)
                    if n == ACCT_AT:
                        make_accT(b)
                    if n == XT_AT:
                        make_xT(b + 1)
                    if n == Q_AT:
                        make_q_logits(b + 1, (ln2_step, b * LN2 + LN2))
                    if n == K_AT:
                        make_k(b + 1)
                    if n == UP0_AT:
                        up(b + 1, 0, (o_out, b * PL + PL - 1))

            setup()
            make_xT(0)
            make_q_logits(0)
            make_k(0)
            pe.wait_ge(w_ready[0], 2)
            up(0, 0)
            turn(0, True)
            with pe.Fori(1, NB) as i:
                turn(i, False)
            attn_out(NB - 1, (qk_split, NB * 4 + 4))


def kernel(**inputs):
    import concourse.bacc as _bacc
    from concourse import mybir as _mybir
    from concourse.bass_utils import run_bass_kernel_spmd as _run

    a = {n: np.ascontiguousarray(v) for n, v in inputs.items()}
    chan = np.arange(D).reshape(4, PL, HD).transpose(2, 1, 0).reshape(-1)
    laid = {
        "x": a["L0_attn_x"],
        "wq": a["L0_attn_Wq"][:, chan], "bq": a["L0_attn_bq"][chan].reshape(D, 1),
        "wk": a["L0_attn_Wk"], "bk": a["L0_attn_bk"].reshape(D, 1),
        "wv": a["L0_attn_Wv"], "bv": a["L0_attn_bv"].reshape(D, 1),
        "wl": a["L0_attn_Wl"], "wlp": a["L0_attn_Wl"][:, chan],
        "bl": a["L0_attn_bl"], "blp": a["L0_attn_bl"][chan].reshape(D, 1),
        "wo": a["L0_attn_Wo"][chan, :], "bo": a["L0_attn_bo"],
        "gate_w": a["L0_ffn_gate_w"], "gate_b": a["L0_ffn_gate_b"],
        "w1": a["L0_ffn_w1"], "b1t": a["L0_ffn_b1"].reshape(NCH, P).T,
        "w2": a["L0_ffn_w2"], "b2t": a["L0_ffn_b2"].T,
        "ln_g": a["L0_ffn_ln_g"], "ln_b": a["L0_ffn_ln_b"],
    }
    nc = _bacc.Bacc("TRN2", target_bir_lowering=False, num_devices=1)
    arrays, args = {}, []
    for name, v in laid.items():
        v = np.ascontiguousarray(v)
        arrays["in_" + name] = v
        args.append(nc.dram_tensor("in_" + name, v.shape, _mybir.dt.from_np(v.dtype), kind="ExternalInput").ap())
    out = nc.dram_tensor("out", a["L0_attn_x"].shape, _mybir.dt.float32, kind="ExternalOutput").ap()
    build(nc, *args, out)
    r = _run(nc, [arrays], core_ids=[0])
    return r.results[0]["out"]
```
